# Optimizing a Trainium2 kernel written in Bass

```python
import numpy as np
import jax
import jax.numpy as jnp

def _softmax(x, axis=-1):
    return jax.nn.softmax(x, axis=axis)

def _gelu(x):
    return jax.nn.gelu(x, approximate=True)

def _silu(x):
    return jax.nn.silu(x)

def _sigmoid(x):
    return jax.nn.sigmoid(x)

def _layernorm(x, axis=-1, eps=1e-05):
    m = jnp.mean(x, axis=axis, keepdims=True)
    v = jnp.var(x, axis=axis, keepdims=True)
    return (x - m) / jnp.sqrt(v + eps)

def _scatter_add(tgt, idx, src, axis=0):
    return tgt.at[idx].add(src)

def _segment_sum(src, seg, n):
    return jax.ops.segment_sum(src, seg, n)
kernel_name = 'mk_decoder_preln_d1_seqx_r4_ae3bd0'

def setup_inputs(seed: int=0):
    np.random.seed(seed)
    _w = jnp.asarray

    def _rec_inputs():
        import jax
        import jax.numpy as jnp
        _rk = jax.random.key(seed)
        x = -0.0002928 + 1 * jax.random.normal(jax.random.fold_in(_rk, 1), (8, 256, 256), jnp.float32)
        _lenS = 256 - jax.random.randint(jax.random.fold_in(_rk, 7), (8,), 0, max(1, 256 // 4) + 1, jnp.int32)
        _lenS2 = 77 - jax.random.randint(jax.random.fold_in(_rk, 8), (8,), 0, max(1, 77 // 4) + 1, jnp.int32)
        _ctx_1024P = jax.random.normal(jax.random.fold_in(_rk, 11), (8, 16, 256), jnp.float32)
        _ctx_1024c = jax.random.dirichlet(jax.random.fold_in(_rk, 511), 0.3 * jnp.ones((16,), jnp.float32), (8, 77))
        _ctx_1024t = jnp.einsum('bsk,bkd->bsd', _ctx_1024c, _ctx_1024P)
        _ctx_1024t = _ctx_1024t * jax.lax.rsqrt(jnp.mean(jnp.square(_ctx_1024t)) + 1e-12) * 0.953939
        ctx_1024 = -1.39393e-06 + 0.999914 * (_ctx_1024t + 0.3 * jax.random.normal(jax.random.fold_in(_rk, 611), (8, 77, 256), jnp.float32))
        _validS = jnp.arange(256)[None, :] < _lenS[:, None]
        _validS2 = jnp.arange(77)[None, :] < _lenS2[:, None]
        _causal = jnp.tril(jnp.ones((256, 256), dtype=bool))
        mask_BxSxS2_bk1 = jnp.broadcast_to(_validS2[:, None, :], (8, 256, 77))
        return (x, ctx_1024, mask_BxSxS2_bk1)
    x, ctx_1024, mask_BxSxS2_bk1 = _rec_inputs()

    def _L0_attn_setup():
        import jax, jax.numpy as jnp
        import numpy as np
        B, T, D, H = (2, 512, 256, 16)
        DH = D // H
        ROPE_BASE = 10000.0

        def _rope(Xh, cos, sin):
            x0 = Xh[..., 0::2]
            x1 = Xh[..., 1::2]
            r0 = cos * x0 - sin * x1
            r1 = sin * x0 + cos * x1
            return jnp.stack((r0, r1), axis=-1).reshape(Xh.shape)
        key = jax.random.key(seed)
        ks = jax.random.split(key, 5)
        s = 1.0 / np.sqrt(D)
        return {'X': jax.random.normal(ks[0], (B, T, D), dtype=jnp.float32), 'W_q': jax.random.normal(ks[1], (D, D), dtype=jnp.float32) * s, 'W_k': jax.random.normal(ks[2], (D, D), dtype=jnp.float32) * s, 'W_v': jax.random.normal(ks[3], (D, D), dtype=jnp.float32) * s, 'W_o': jax.random.normal(ks[4], (D, D), dtype=jnp.float32) * s}
    _L0_attn_all = _L0_attn_setup()
    _L0_attn_in = {k: v for k, v in _L0_attn_all.items() if k in ('W_q', 'W_k', 'W_v', 'W_o')}
    del _L0_attn_all

    def _L0_xattn_setup():
        import jax, jax.numpy as jnp
        import numpy as np
        B, S, D_MODEL, N_HEADS, D_K, D_V = (2, 512, 256, 16, 64, 64)
        key = jax.random.key(seed)
        k1, k2, k3, k4, k5, k6, k7 = jax.random.split(key, 7)
        scale = 1.0 / np.sqrt(D_MODEL)
        inputs = {'input_Q': jax.random.normal(k1, (B, S, D_MODEL), dtype=jnp.float32), 'input_K': jax.random.normal(k2, (B, S, D_MODEL), dtype=jnp.float32), 'input_V': jax.random.normal(k3, (B, S, D_MODEL), dtype=jnp.float32), 'attn_mask': jnp.broadcast_to(~jnp.tril(jnp.ones((S, S), dtype=bool)), (B, S, S)), 'flag': 0, 'W_Q': jax.random.normal(k4, (D_MODEL, N_HEADS * D_K), dtype=jnp.float32) * scale, 'W_K': jax.random.normal(k5, (D_MODEL, N_HEADS * D_K), dtype=jnp.float32) * scale, 'W_V': jax.random.normal(k6, (D_MODEL, N_HEADS * D_V), dtype=jnp.float32) * scale, 'W_O': jax.random.normal(k7, (N_HEADS * D_V, D_MODEL), dtype=jnp.float32) * scale}
        return inputs
    _L0_xattn_all = _L0_xattn_setup()
    _L0_xattn_in = {k: v for k, v in _L0_xattn_all.items() if k in ('W_Q', 'W_K', 'W_V', 'W_O')}
    del _L0_xattn_all

    def _L0_ffn_setup():
        import jax, jax.numpy as jnp
        import numpy as np
        BITS = 8
        LORA_RANK = 16
        LORA_ALPHA = 32
        SCALING = LORA_ALPHA / LORA_RANK

        def fake_quant_weight(w, bits=BITS):
            qmax = 2.0 ** (bits - 1) - 1
            scale = jnp.max(jnp.abs(w)) / qmax
            wq = jnp.clip(jnp.round(w / scale), -qmax - 1, qmax) * scale
            return w + jax.lax.stop_gradient(wq - w)

        def qat_lora_linear(x, W, b, A, B):
            Wq = fake_quant_weight(W)
            base = jnp.einsum('bsi,oi->bso', x, Wq) + b
            lora = jnp.einsum('bsr,or->bso', jnp.einsum('bsi,ri->bsr', x, A), B)
            return base + SCALING * lora
        key = jax.random.key(seed)
        ks = jax.random.split(key, 9)
        d, f = (256, 1024)
        s_in = 1.0 / np.sqrt(d)
        s_ff = 1.0 / np.sqrt(f)
        return {'hidden_states': jax.random.normal(ks[0], (4, 512, d), jnp.float32), 'W_fc': jax.random.normal(ks[1], (f, d), jnp.float32) * s_in, 'b_fc': jnp.zeros((f,), jnp.float32), 'A_fc': jax.random.normal(ks[2], (LORA_RANK, d), jnp.float32) * s_in, 'B_fc': jnp.zeros((f, LORA_RANK), jnp.float32), 'W_proj': jax.random.normal(ks[3], (d, f), jnp.float32) * s_ff, 'b_proj': jnp.zeros((d,), jnp.float32), 'A_proj': jax.random.normal(ks[4], (LORA_RANK, f), jnp.float32) * s_ff, 'B_proj': jnp.zeros((d, LORA_RANK), jnp.float32)}
    _L0_ffn_all = _L0_ffn_setup()
    _L0_ffn_in = {k: v for k, v in _L0_ffn_all.items() if k in ('W_fc', 'b_fc', 'A_fc', 'B_fc', 'W_proj', 'b_proj', 'A_proj', 'B_proj')}
    del _L0_ffn_all
    return {'x': x, 'ctx_1024': ctx_1024, 'mask_BxSxS2_bk1': mask_BxSxS2_bk1, 'L0_attn_W_q': _L0_attn_in['W_q'], 'L0_attn_W_k': _L0_attn_in['W_k'], 'L0_attn_W_v': _L0_attn_in['W_v'], 'L0_attn_W_o': _L0_attn_in['W_o'], 'L0_xattn_W_Q': _L0_xattn_in['W_Q'], 'L0_xattn_W_K': _L0_xattn_in['W_K'], 'L0_xattn_W_V': _L0_xattn_in['W_V'], 'L0_xattn_W_O': _L0_xattn_in['W_O'], 'L0_ffn_W_fc': _L0_ffn_in['W_fc'], 'L0_ffn_b_fc': _L0_ffn_in['b_fc'], 'L0_ffn_A_fc': _L0_ffn_in['A_fc'], 'L0_ffn_B_fc': _L0_ffn_in['B_fc'], 'L0_ffn_W_proj': _L0_ffn_in['W_proj'], 'L0_ffn_b_proj': _L0_ffn_in['b_proj'], 'L0_ffn_A_proj': _L0_ffn_in['A_proj'], 'L0_ffn_B_proj': _L0_ffn_in['B_proj']}

def reference(x, ctx_1024, mask_BxSxS2_bk1, L0_attn_W_q, L0_attn_W_k, L0_attn_W_v, L0_attn_W_o, L0_xattn_W_Q, L0_xattn_W_K, L0_xattn_W_V, L0_xattn_W_O, L0_ffn_W_fc, L0_ffn_b_fc, L0_ffn_A_fc, L0_ffn_B_fc, L0_ffn_W_proj, L0_ffn_b_proj, L0_ffn_A_proj, L0_ffn_B_proj):
    import jax
    import jax.numpy as jnp

    def _L0_attn_ref(X, W_q, W_k, W_v, W_o):
        import jax, jax.numpy as jnp
        import numpy as np
        B, T, D, H = (2, 512, 256, 16)
        DH = D // H
        ROPE_BASE = 10000.0

        def _rope(Xh, cos, sin):
            x0 = Xh[..., 0::2]
            x1 = Xh[..., 1::2]
            r0 = cos * x0 - sin * x1
            r1 = sin * x0 + cos * x1
            return jnp.stack((r0, r1), axis=-1).reshape(Xh.shape)
        b, t, d = X.shape
        Q = X @ W_q.T
        K = X @ W_k.T
        V = X @ W_v.T
        Qh = Q.reshape(b, t, H, DH).transpose(0, 2, 1, 3)
        Kh = K.reshape(b, t, H, DH).transpose(0, 2, 1, 3)
        Vh = V.reshape(b, t, H, DH).transpose(0, 2, 1, 3)
        theta = ROPE_BASE ** (-2.0 * jnp.arange(DH // 2, dtype=jnp.float32) / DH)
        pos = jnp.arange(t, dtype=jnp.float32)
        angles = pos[:, None] * theta[None, :]
        cos = jnp.cos(angles).astype(Qh.dtype)
        sin = jnp.sin(angles).astype(Qh.dtype)
        Qr = _rope(Qh, cos, sin)
        Kr = _rope(Kh, cos, sin)
        scores = jnp.einsum('bhqd,bhkd->bhqk', Qr, Kr) * DH ** (-0.5)
        causal = jnp.triu(jnp.ones((t, t), dtype=bool), 1)
        neg = jnp.finfo(scores.dtype).min
        scores = jnp.where(causal[None, None], neg, scores)
        pattern = jax.nn.softmax(scores, axis=-1)
        heads = jnp.einsum('bhqk,bhkd->bhqd', pattern, Vh)
        out = heads.transpose(0, 2, 1, 3).reshape(b, t, d)
        return out @ W_o.T

    def _L0_xattn_ref(input_Q, input_K, input_V, attn_mask, flag, W_Q, W_K, W_V, W_O):
        import jax, jax.numpy as jnp
        import numpy as np
        B, S, D_MODEL, N_HEADS, D_K, D_V = (2, 512, 256, 16, 64, 64)
        b = input_Q.shape[0]
        Q = (input_Q @ W_Q).reshape(b, -1, N_HEADS, D_K).transpose(0, 2, 1, 3)
        K = (input_K @ W_K).reshape(b, -1, N_HEADS, D_K).transpose(0, 2, 1, 3)
        V = (input_V @ W_V).reshape(b, -1, N_HEADS, D_V).transpose(0, 2, 1, 3)
        scores = jnp.einsum('bhqd,bhkd->bhqk', Q, K) / np.sqrt(D_K).astype(np.float32)
        scores = jnp.where(attn_mask[:, None, :, :], jnp.float32(-1000000000.0), scores)
        attn = jax.nn.softmax(scores, axis=-1)
        context = jnp.einsum('bhqk,bhkd->bhqd', attn, V)
        context = context.transpose(0, 2, 1, 3).reshape(b, -1, N_HEADS * D_V)
        return context @ W_O

    def _L0_ffn_ref(hidden_states, W_fc, b_fc, A_fc, B_fc, W_proj, b_proj, A_proj, B_proj):
        import jax, jax.numpy as jnp
        import numpy as np
        BITS = 8
        LORA_RANK = 16
        LORA_ALPHA = 32
        SCALING = LORA_ALPHA / LORA_RANK

        def fake_quant_weight(w, bits=BITS):
            qmax = 2.0 ** (bits - 1) - 1
            scale = jnp.max(jnp.abs(w)) / qmax
            wq = jnp.clip(jnp.round(w / scale), -qmax - 1, qmax) * scale
            return w + jax.lax.stop_gradient(wq - w)

        def qat_lora_linear(x, W, b, A, B):
            Wq = fake_quant_weight(W)
            base = jnp.einsum('bsi,oi->bso', x, Wq) + b
            lora = jnp.einsum('bsr,or->bso', jnp.einsum('bsi,ri->bsr', x, A), B)
            return base + SCALING * lora
        h = qat_lora_linear(hidden_states, W_fc, b_fc, A_fc, B_fc)
        h = jax.nn.gelu(h, approximate=False)
        h = qat_lora_linear(h, W_proj, b_proj, A_proj, B_proj)
        return h
    x = x + _L0_attn_ref(_layernorm(x, axis=-1), L0_attn_W_q, L0_attn_W_k, L0_attn_W_v, L0_attn_W_o)
    x = x + _L0_xattn_ref(_layernorm(x, axis=-1), ctx_1024, ctx_1024, mask_BxSxS2_bk1, 0, L0_xattn_W_Q, L0_xattn_W_K, L0_xattn_W_V, L0_xattn_W_O)
    x = x + _L0_ffn_ref(_layernorm(x, axis=-1), L0_ffn_W_fc, L0_ffn_b_fc, L0_ffn_A_fc, L0_ffn_B_fc, L0_ffn_W_proj, L0_ffn_b_proj, L0_ffn_A_proj, L0_ffn_B_proj)
    return x

_drawn_inputs = setup_inputs


def setup_inputs(seed=0):
    import zlib

    import numpy as np

    out = dict(_drawn_inputs(seed))
    spreads = {'L0_ffn_b_fc': (0.0, 0.1),
     'L0_ffn_B_fc': (0.0, 0.1),
     'L0_ffn_b_proj': (0.0, 0.1),
     'L0_ffn_B_proj': (0.0, 0.1)}
    factors = {}
    for name, (base, spread) in spreads.items():
        noise = np.random.default_rng([zlib.crc32(name.encode()), seed]).standard_normal(out[name].shape)
        drawn = base * np.exp(spread * noise) if base else spread * noise
        out[name] = jnp.asarray(drawn.astype(out[name].dtype))
    for name, factor in factors.items():
        out[name] = (out[name] * factor).astype(out[name].dtype)
    return out
```

```python
from contextlib import ExitStack

import numpy as np

import concourse.bass as bass
from concourse import mybir

P = 128
F32 = mybir.dt.float32
F32R = mybir.dt.float32r
BF16 = mybir.dt.bfloat16
U8 = mybir.dt.uint8
ALU = mybir.AluOpType
ACT = mybir.ActivationFunctionType
AX_X = mybir.AxisListType.X
RMAX = bass.bass_isa.ReduceOp.max

EPS = 1e-5
QMAX = 127.0
ROUND = 12582912.0
NEG = -float(2.0 ** 100)
LORA_SCALE = 2.0


def decoder_layer(nc, x, ctxT, mask, wqT, wkT, wvT, woT, wQ, wK, wV, wO, wfcT, bfc, Afc, BfcT,
                  wpjT, bpj, Apj, BpjT, cos, sin, out):
    NB, T, D = x.shape
    QT = T // P
    KD = D // P
    H = 16
    DH = D // H
    HH = H // 2
    HI = DH // 2
    S2 = mask.shape[2]
    XD = wQ.shape[1]
    XM = XD // P
    DX = XD // H
    R = Afc.shape[0]
    F = wfcT.shape[1]
    FM = F // P
    PAIR = 2 * S2
    W = 256
    STK = 3 * DH
    SX = STK + 2
    SCALE = float(DH) ** -0.5
    XSCALE = float(DX) ** -0.5

    with ExitStack() as ctx:
        def sb(name, shape, dt=F32):
            return ctx.enter_context(nc.sbuf_tensor(name, shape, dt))

        def sem(name):
            return ctx.enter_context(nc.semaphore(name))

        bank = ctx.enter_context(nc.psum_tensor("banks", [P, 8, 512], F32))

        def halves(b, w=W):
            return bank[:, b, :].rearrange("p (a n) -> p a n", n=w)

        ident = sb("ident", [P, P])
        ident_bf = sb("ident_bf", [P, P], BF16)
        causal_qk = sb("causal_qk", [P, 2, P], BF16)
        causal_kq = sb("causal_kq", [P, 2, P], BF16)
        cos_t = sb("cos_t", [P, T])
        sin_t = sb("sin_t", [P, T])
        bfc_t = sb("bfc_t", [P, FM])
        bpj_t = sb("bpj_t", [P, D])

        def pair(name, shape):
            return sb(name + "_hi", shape, F32R), sb(name + "_lo", shape, F32R)

        wqkv = pair("wqkv", [P, KD, 3 * D])
        wo = pair("wo", [P, KD, D])
        wq2 = pair("wq2", [P, KD, XD])
        wo2 = pair("wo2", [P, XM, D])
        wfc = pair("wfc", [P, KD, F])
        wpj = pair("wpj", [P, FM, D])

        x_in = sb("x_in", [P, QT, D])
        x_res = sb("x_res", [P, QT, D])
        xn_a = sb("xn_a", [P, QT, D])
        st_a = sb("st_a", [P, QT, 6])
        mv_a = sb("mv_a", [P, QT, 2])
        rs_a = sb("rs_a", [P, QT, 1])
        half_a = sb("half_a", [P, QT, 1])
        xaT = pair("xaT", [P, KD, T])
        rot = sb("rot", [P, 2, 2, T])
        rot_s = pair("rot_s", [P, 2, 2, T])
        unnorm = rot[:].rearrange("p a b t -> p (a b) t")
        attn = sb("attn", [P, QT, D])
        attn_s = [v[:, 0] for v in rot_s]
        rc_a = sb("rc_a", [P, QT, H])
        q_stack = sb("q_stack", [P, HH, T], F32R)
        k_stack = sb("k_stack", [P, HH, T], F32R)
        v_aug = sb("v_aug", [P, QT, H, 32])
        probs = sb("probs", [P, 8, 3 * P])
        tcos = probs[:, 0:4, :].rearrange("p a b -> p (a b)")[:, 0:2 * T].rearrange("p (j t) -> p j t", j=2)
        tsin = probs[:, 4:8, :].rearrange("p a b -> p (a b)")[:, 0:2 * T].rearrange("p (j t) -> p j t", j=2)
        mneg = sb("mneg", [P, QT, 2, HH])
        mneg_s = sb("mneg_s", [P, QT, 32], F32R)
        mnegT = sb("mnegT", [32, T], F32R)
        x1 = sb("x1", [P, QT, D])

        x2 = sb("x2", [P, QT, D])
        st_b = sb("st_b", [P, QT, 6])
        mv_b = sb("mv_b", [P, QT, 2])
        rs_b = sb("rs_b", [P, QT, 1])
        xbT = pair("xbT", [P, KD, T])
        q2 = pair("q2", [P, XM, T])
        hid = q2
        KW = (XM - 1) * PAIR + W
        k2 = pair("k2", [P, KW])
        v2 = sb("v2", [S2, XD])
        mask_u8 = sb("mask_u8", [P, QT, S2], U8)
        mask_bf = sb("mask_bf", [P, QT, 2, S2], BF16)
        mx2 = sb("mx2", [P, 2, 4, 2])
        sm2 = sb("sm2", [P, 2, 4, 2])
        rc2 = sb("rc2", [P, 2, 4, 2])
        c2 = pair("c2", [P, 2, T])
        LOAD = KD * XD
        work = sb("work", [P, max(2 * LOAD, 4 * T + 16 * S2 + 3 * QT * D)])
        o = 4 * T
        p2T = work[0:S2, 0:o].rearrange("p (h t) -> p h t", t=T)
        gl = work[:, 0:o].rearrange("p (r a t) -> p r a t", r=2, t=T)
        sc2 = [work[:, o + r * 8 * S2:o + (r + 1) * 8 * S2].rearrange("p (g a s) -> p g a s", g=4, s=S2)
               for r in range(2)]
        o += 16 * S2
        x2b, xn_b, y = (work[:, o + j * QT * D:o + (j + 1) * QT * D].rearrange("p (q d) -> p q d", q=QT)
                        for j in range(3))

        NS = NB * S2
        HS = NS // 2
        LOAD = KD * XD
        raw = [work[:, 0:LOAD], work[:, LOAD:2 * LOAD]]
        kv_w = [v[:].rearrange("p m t -> p (m t)").rearrange("p (k n) -> p k n", k=KD) for v in q2]
        ctx_s = [v[:, 0:KD * NS].rearrange("p (k n) -> p k n", k=KD) for v in k2]
        k_out = [[v[:].rearrange("p a t -> p (a t)")[:, 0:HS] for v in pr] for pr in (c2, xbT)]
        wmax = sb("wmax", [P, 2])
        wscale = sb("wscale", [P, 2])
        winv = sb("winv", [P, 2])

        k2_dram = nc.dram_tensor("k2_dram", [2, P, XM, NS], F32, kind="Internal").ap()
        v2_dram = nc.dram_tensor("v2_dram", [NB, S2, XD], F32, kind="Internal").ap()

        block = ctx.enter_context(nc.Block())

        const_ld, const_ok, k2_zero = sem("const_ld"), sem("const_ok"), sem("k2_zero")
        raw_ld = [sem(f"raw{r}_ld") for r in range(2)]
        w_hi, w_lo = sem("w_hi"), sem("w_lo")
        kx_ps, kx_hi, kx_lo, kx_st = sem("kx_ps"), sem("kx_hi"), sem("kx_lo"), [sem(f"kx_st{r}") for r in range(2)]
        vx_ps, vx_ok, vx_st = sem("vx_ps"), sem("vx_ok"), [sem(f"vx_st{r}") for r in range(2)]
        lora_ld, lora_ps = sem("lora_ld"), sem("lora_ps")
        wmax_ok, wmax_all, wstep = sem("wmax_ok"), sem("wmax_all"), sem("wstep")
        waited_sp, waited_dve = sem("waited_sp"), sem("waited_dve")
        x_ld, xres_ld = sem("x_ld"), sem("xres_ld")
        lna_st, lna_mv, lna_rs, xn_a_ok = sem("lna_st"), sem("lna_mv"), sem("lna_rs"), sem("xn_a_ok")
        xaT_ps, xaT_hi, xaT_lo = sem("xaT_ps"), sem("xaT_hi"), sem("xaT_lo")
        qk_ps, v_ps, v_ok = sem("qk_ps"), sem("v_ps"), sem("v_ok")
        trig, rot_ok, rot_hi, rot_lo = sem("trig"), sem("rot_ok"), sem("rot_hi"), sem("rot_lo")
        stack_ld, shift_ld = sem("stack_ld"), sem("shift_ld")
        s_ps, s_max = sem("s_ps"), sem("s_max")
        m_split, mT_ps, mT_ok = sem("m_split"), sem("mT_ps"), sem("mT_ok")
        st_ps, p_ok, pv_ps = sem("st_ps"), sem("p_ok"), sem("pv_ps")
        u_ok, ut_ps, rca_ok, att_ok = sem("u_ok"), sem("ut_ps"), sem("rca_ok"), sem("att_ok")
        atT_ps, att_hi, att_lo = sem("atT_ps"), sem("att_hi"), sem("att_lo")
        lna_ve, lnb_ve = sem("lna_ve"), sem("lnb_ve")
        o_ps, x1_ok = sem("o_ps"), sem("x1_ok")
        lnb_st, lnb_mv, lnb_rs, xn_b_ok = sem("lnb_st"), sem("lnb_mv"), sem("lnb_rs"), sem("xn_b_ok")
        xbT_ps, xbT_hi, xbT_lo = sem("xbT_ps"), sem("xbT_hi"), sem("xbT_lo")
        mask_ld, mask_ok, k2_ld, v2_ld = sem("mask_ld"), sem("mask_ok"), sem("k2_ld"), sem("v2_ld")
        q2_ps, q2_hi, q2_lo = sem("q2_ps"), sem("q2_hi"), sem("q2_lo")
        s2_ps, mx2_ok, sub_ok, e2_ok = sem("s2_ps"), sem("mx2_ok"), sem("sub_ok"), sem("e2_ok")
        sm2_ok, rc2_ok, nrm_ok = sem("sm2_ok"), sem("rc2_ok"), sem("nrm_ok")
        t2_ps, p2T_ok, c2_ps, c2_hi, c2_lo = (sem(n) for n in ("t2_ps", "p2T_ok", "c2_ps", "c2_hi", "c2_lo"))
        o2_ps, x2_ok, x2b_ok = sem("o2_ps"), sem("x2_ok"), sem("x2b_ok")
        fc_ps, gl_ok, hid_hi, hid_lo = sem("fc_ps"), sem("gl_ok"), sem("hid_hi"), sem("hid_lo")
        y_ps, y_ok, y_st = sem("y_ps"), sem("y_ok"), sem("y_st")

        def elements(step):
            def run(eng):
                step(0, None)
                step(1, 0)
                with eng.Fori(2, NB) as i:
                    step(i, i - 1)
                step(None, NB - 1)
            return run

        N_CONST = 5
        QKV_W, WO_W, WK_W, CTX_W, WV_W, WQ_W, WO2_W, FC_W, PJ_W = range(9)
        split_to = [[v[:].rearrange("p k n -> p (k n)") for v in wqkv],
                    [v[:].rearrange("p k n -> p (k n)") for v in wo],
                    [v.rearrange("p k n -> p (k n)") for v in kv_w],
                    [v[:, 0:KD * NS] for v in k2],
                    [v.rearrange("p k n -> p (k n)") for v in kv_w]] + [
                    [v[:].rearrange("p k n -> p (k n)") for v in pr] for pr in (wq2, wo2, wfc, wpj)]
        raw_of = [raw[k % 2][:, 0:split_to[k][0].shape[1]] for k in range(9)]
        RAW_DMAS = [3, 1, 1, 1, 1, 1, 1, 1, 1]
        raw_count = [16 * sum(RAW_DMAS[j] for j in range(k % 2, k + 1, 2)) for k in range(9)]

        @block.sync
        def _(sp):
            def load_raw(k, *views):
                if k >= 2:
                    sp.wait_ge(w_lo, k - 1)
                for dst, src in views:
                    sp.dma_start(dst, src).then_inc(raw_ld[k % 2], 16)

            def tiles(k, n):
                return raw_of[k].rearrange("p (k n) -> p k n", n=n)

            def rows(w):
                return w.rearrange("(k p) n -> p k n", p=P)

            sp.dma_start(x_in[:], x[0].rearrange("(q p) d -> p q d", p=P)).then_inc(x_ld, 16)
            load_raw(QKV_W, *[(tiles(QKV_W, 3 * D)[:, :, j * D:(j + 1) * D], rows(w))
                              for j, w in enumerate((wqT, wkT, wvT))])
            sp.dma_start(cos_t[:], cos).then_inc(const_ld, 16)
            sp.dma_start(sin_t[:], sin).then_inc(const_ld, 16)
            sp.dma_start(bfc_t[:], bfc).then_inc(const_ld, 16)
            sp.dma_start(bpj_t[:], bpj.broadcast_to([P, D])).then_inc(const_ld, 16)
            load_raw(WO_W, (tiles(WO_W, D), rows(woT)))
            load_raw(WK_W, (tiles(WK_W, XD), rows(wK)))
            load_raw(CTX_W, (tiles(CTX_W, NS), rows(ctxT)))
            load_raw(WV_W, (tiles(WV_W, XD), rows(wV)))
            n = 0
            for m in range(XM):
                for half in range(2):
                    sp.wait_ge(kx_hi, n + 1)
                    sp.wait_ge(kx_lo, n + 1)
                    for piece in range(2):
                        sp.dma_start(k2_dram[piece, :, m, half * HS:(half + 1) * HS],
                                     k_out[n % 2][piece].bitcast(F32)).then_inc(kx_st[n % 2], 16)
                    n += 1
            load_raw(WQ_W, (tiles(WQ_W, XD), rows(wQ)))
            n = 0
            for b in range(NB):
                for half in range(2):
                    sp.wait_ge(vx_ok, n + 1)
                    sp.dma_start(v2_dram[b, :, half * 512:(half + 1) * 512],
                                 v2[:, half * 512:(half + 1) * 512]).then_inc(vx_st[n % 2], 16)
                    n += 1
            load_raw(WO2_W, (tiles(WO2_W, D), rows(wO)))
            load_raw(FC_W, (tiles(FC_W, F), rows(wfcT)))
            sp.dma_start(x2[0:R, 0, :], Afc).then_inc(lora_ld, 16)
            sp.dma_start(x2[0:R, 1, :], BpjT).then_inc(lora_ld, 16)
            for r in range(2):
                sp.wait_ge(vx_st[r], 16 * NB)
            sp.dma_start(v2[0:R, :], BfcT).then_inc(lora_ld, 16)
            load_raw(PJ_W, (tiles(PJ_W, D), rows(wpjT)))
            sp.wait_ge(lora_ps, 1)
            sp.dma_start(v2[0:R, :], Apj).then_inc(lora_ld, 16)
            for r in range(2):
                sp.wait_ge(kx_st[r], 16 * 2 * XM)
            sp.wait_ge(lora_ps, 2)
            sp.wait_ge(k2_zero, 1)

            def step(a, b):
                if a is not None and b is not None:
                    sp.wait_ge(xn_a_ok, a)
                    sp.sem_inc(waited_sp, 1)
                    sp.dma_start(x_in[:], x[a].rearrange("(q p) d -> p q d", p=P)).then_inc(x_ld, 16)
                if b is not None:
                    sp.wait_ge(mask_ok, b)
                    sp.sem_inc(waited_sp, 1)
                    sp.dma_start(mask_u8[:], mask[b].rearrange("(q p) s -> p q s", p=P)).then_inc(mask_ld, 16)
                    sp.wait_ge(s2_ps, 4 * b)
                    sp.sem_inc(waited_sp, 1)
                    for piece in range(2):
                        for p in range(2):
                            dst = k2[piece][64 * p:64 * p + DX, 0:XM * PAIR].bitcast(F32)
                            sp.dma_start(
                                dst.rearrange("p (m a s) -> p m a s", a=2, s=S2)[:, :, p, :],
                                k2_dram[piece, 64 * p:64 * p + DX].rearrange("p m (b s) -> p m b s", s=S2)[:, :, b, :]
                            ).then_inc(k2_ld, 16)
                    sp.wait_ge(c2_ps, 4 * b)
                    sp.sem_inc(waited_sp, 1)
                    sp.dma_start(v2[:], v2_dram[b]).then_inc(v2_ld, 16)
                if a is not None:
                    for w, (stack, order) in enumerate(((q_stack, (0, 0, 1)), (k_stack, (0, 1, 0)))):
                        if w == 0:
                            sp.wait_ge(st_ps, H * a)
                        sp.wait_ge(rot_hi, 2 * a + w + 1)
                        sp.wait_ge(rot_lo, 2 * a + w + 1)
                        for p in range(2):
                            for c, piece in enumerate(order):
                                for j in range(2):
                                    row = 64 * p + c * DH + j * HI
                                    sp.dma_start(stack[row:row + HI, :, :].bitcast(F32),
                                                 rot_s[piece][64 * p:64 * p + 64, w, j, :].bitcast(F32)
                                                 ).then_inc(stack_ld, 16)
                    sp.wait_ge(x1_ok, a)
                    sp.sem_inc(waited_sp, 1)
                    sp.dma_start(x_res[:], x[a].rearrange("(q p) d -> p q d", p=P)).then_inc(xres_ld, 16)
                    sp.wait_ge(mT_ok, a + 1)
                    for p in range(2):
                        for piece in range(2):
                            row = 64 * p + STK + piece
                            sp.dma_start(q_stack[row:row + 1, :, :].bitcast(F32),
                                         mnegT[piece * H + p * HH:piece * H + (p + 1) * HH, :].bitcast(F32)
                                         ).then_inc(shift_ld, 16)

            elements(step)(sp)

        @block.gpsimd
        def _(pool):
            pool.memset(ident[:], 0.0)
            pool.memset(causal_qk[:], 0.0)
            pool.memset(causal_kq[:], 0.0).then_inc(const_ok, 1)
            pool.wait_ge(const_ok, 1)
            pool.affine_select(out=ident[:], in_=ident[:], compare_op=ALU.not_equal, fill=1.0, base=0,
                               pattern=[[-1, P]], channel_multiplier=1).then_inc(const_ok, 1)
            pool.affine_select(out=causal_qk[:], in_=causal_qk[:], compare_op=ALU.is_ge, fill=NEG, base=0,
                               pattern=[[0, 2], [-1, P]], channel_multiplier=1).then_inc(const_ok, 1)
            pool.affine_select(out=causal_kq[:], in_=causal_kq[:], compare_op=ALU.is_ge, fill=NEG, base=0,
                               pattern=[[0, 2], [1, P]], channel_multiplier=-1).then_inc(const_ok, 1)
            pool.wait_ge(const_ok, 2)
            pool.tensor_copy(ident_bf[:], ident[:]).then_inc(const_ok, 1)
            pool.memset(half_a[:], -0.5)
            pool.memset(v_aug[:], 0.0).then_inc(const_ok, 1)
            pool.wait_ge(const_ok, 6)
            pool.memset(v_aug[:, :, :, DH:DH + 1], 1.0).then_inc(const_ok, 1)
            pool.memset(k_stack[:].bitcast(F32), 1.0).then_inc(const_ok, 1)
            for n in range(2):
                pool.wait_ge(wmax_ok, n + 1)
                pool.partition_all_reduce(wmax[:, 1:2], wmax[:, 0:1], P, RMAX).then_inc(wmax_all, 1)
                pool.wait_ge(wstep, 6 * n + 1)
            pool.wait_ge(vx_ps, 2 * NB)
            for v in k2:
                last = pool.memset(v[:].bitcast(F32), 0.0)
            last.then_inc(k2_zero, 1)

            def rotate(a, w):
                pool.wait_ge(trig, 2 * a + w + 1)
                if w == 0:
                    pool.wait_ge(ut_ps, a)
                pool.tensor_tensor(rot[:, w, 0, :], tcos[:, 0, :], tsin[:, 1, :], ALU.subtract)
                pool.tensor_tensor(rot[:, w, 1, :], tcos[:, 1, :], tsin[:, 0, :], ALU.add).then_inc(rot_ok, 1)
                pool.wait_ge(rot_hi, 2 * a + w + 1)
                pool.wait_ge(rot_ok, 2 * a + w + 1)
                pool.tensor_tensor(rot_s[1][:, w], rot[:, w], rot_s[0][:, w].bitcast(F32),
                                   ALU.subtract).then_inc(rot_lo, 1)

            def inverse_deviation(rs, ve_ok, rs_ok, n):
                pool.wait_ge(ve_ok, n + 1)
                pool.tensor_tensor(rs[:], rs[:], half_a[:], ALU.pow).then_inc(rs_ok, 1)

            def normalise(b, g):
                pool.wait_ge(rc2_ok, 4 * b + g + 1)
                pool.tensor_tensor(sc2[g % 2], sc2[g % 2],
                                   rc2[:, g % 2].rearrange("p g a -> p g a ()").broadcast_to([P, 4, 2, S2]),
                                   ALU.mult).then_inc(nrm_ok, 1)

            def residual_bias(b):
                pool.wait_ge(x2_ok, b + 1)
                pool.wait_ge(y_ok, b)
                for q in range(QT):
                    last = pool.tensor_tensor(x2b[:, q, :], x2[:, q, :], bpj_t[:], ALU.add)
                last.then_inc(x2b_ok, 1)

            def hidden_lo(b, g):
                pool.wait_ge(hid_hi, 4 * b + g + 1)
                pool.tensor_tensor(hid[1][:, 2 * g:2 * g + 2], gl[:, g % 2],
                                   hid[0][:, 2 * g:2 * g + 2].bitcast(F32), ALU.subtract).then_inc(hid_lo, 1)

            def step(a, b):
                if a is not None:
                    inverse_deviation(rs_a, lna_ve, lna_rs, a)
                if b is not None:
                    inverse_deviation(rs_b, lnb_ve, lnb_rs, 2 * b)
                if a is not None:
                    rotate(a, 0)
                    rotate(a, 1)
                if b is not None:
                    for g in range(4):
                        normalise(b, g)
                if b is not None:
                    inverse_deviation(rs_b, lnb_ve, lnb_rs, 2 * b + 1)
                    residual_bias(b)
                    for g in range(4):
                        hidden_lo(b, g)
                    pool.wait_ge(y_ok, b + 1)
                    pool.dma_start(out[b].rearrange("(q p) d -> p q d", p=P), y).then_inc(y_st, 16)

            elements(step)(pool)
            pool.wait_ge(y_st, 16 * NB)

        @block.tensor
        def _(pe):
            def product(dst, w, x_, first, last, **kw):
                pe.matmul(dst, w[0], x_[0], start=first, stop=False, **kw)
                pe.matmul(dst, w[0], x_[1], start=False, stop=False, **kw)
                return pe.matmul(dst, w[1], x_[0], start=False, stop=last, **kw)

            def both(pr, *index):
                return [v[index] for v in pr]

            def start_b():
                n = 0
                pe.wait_ge(w_lo, CTX_W + 1)
                for m in range(XM):
                    for half in range(2):
                        if n >= 4:
                            pe.wait_ge(kx_lo, n - 3)
                        for k in range(KD):
                            mm = product(bank[:, 4 + n % 4, 0:HS], both(kv_w, slice(None), k, slice(m * P, m * P + P)),
                                         both(ctx_s, slice(None), k, slice(half * HS, (half + 1) * HS)),
                                         k == 0, k == KD - 1)
                        mm.then_inc(kx_ps, 1)
                        n += 1
                pe.wait_ge(w_lo, WV_W + 1)
                for r in range(2):
                    pe.wait_ge(kx_lo, 2 * XM)
                n = 0
                for b in range(NB):
                    for half in range(2):
                        if n >= 4:
                            pe.wait_ge(vx_ok, n - 3)
                        for k in range(KD):
                            mm = product(bank[0:S2, 4 + n % 4, :], both(ctx_s, slice(None), k, slice(b * S2, (b + 1) * S2)),
                                         both(kv_w, slice(None), k, slice(half * 512, (half + 1) * 512)),
                                         k == 0, k == KD - 1)
                        mm.then_inc(vx_ps, 1)
                        n += 1
                pe.wait_ge(vx_ok, 2 * NB)
                pe.wait_ge(lora_ld, 16 * 3)
                for k in range(KD):
                    for half in range(2):
                        mm = pe.matmul(bank[:, 4 + 2 * k + half, :], x2[0:R, 0, k * P:(k + 1) * P],
                                       v2[0:R, half * 512:(half + 1) * 512], start=True, stop=True)
                mm.then_inc(lora_ps, 1)
                pe.wait_ge(lora_ld, 16 * 4)
                pe.wait_ge(wstep, 6)
                for m in range(FM):
                    mm = pe.matmul(bank[:, 4 + m // 2, (m % 2) * D:(m % 2 + 1) * D], v2[0:R, m * P:(m + 1) * P],
                                   x2[0:R, 1, :], start=True, stop=True)
                mm.then_inc(lora_ps, 1)
                pe.wait_ge(wstep, 12)

            def transpose_a(a):
                pe.wait_ge(xn_a_ok, a + 1)
                pe.wait_ge(x1_ok, a)
                for k in range(KD):
                    for q in range(QT):
                        mm = pe.transpose(bank[:, 0, k * T + q * P:k * T + (q + 1) * P],
                                          xn_a[:, q, k * P:(k + 1) * P], ident[:])
                mm.then_inc(xaT_ps, 1)

            def project(a):
                pe.wait_ge(xaT_hi, a + 1)
                pe.wait_ge(xaT_lo, a + 1)
                for w in range(2):
                    if w == 0:
                        pe.wait_ge(p_ok, H * a)
                    else:
                        pe.wait_ge(att_lo, a)
                    for j in range(2):
                        for k in range(KD):
                            mm = product(halves(1 + w)[:, j, :],
                                         both(wqkv, slice(None), k, slice(w * D + j * P, w * D + (j + 1) * P)),
                                         both(xaT, slice(None), k), k == 0, k == KD - 1)
                    mm.then_inc(qk_ps, 1)
                for q in range(QT):
                    for k in range(KD):
                        mm = product(halves(3)[:, q, :], both(xaT, slice(None), k, slice(q * P, (q + 1) * P)),
                                     both(wqkv, slice(None), k, slice(2 * D, 3 * D)), k == 0, k == KD - 1)
                mm.then_inc(v_ps, 1)

            def scores(a, g):
                if g == 0:
                    pe.wait_ge(stack_ld, 16 * 24 * (a + 1))
                    pe.wait_ge(trig, 2 * a + 1)
                elif g == 1:
                    pe.wait_ge(trig, 2 * a + 2)
                    pe.wait_ge(v_ok, a + 1)
                else:
                    pe.wait_ge(s_max, 8 * a + g - 1)
                for p in range(2):
                    bk = 2 * (g % 2) + p
                    pe.matmul(bank[:, bk, P:3 * P], ident_bf[:], causal_qk[:].rearrange("p a n -> p (a n)"),
                              start=True, stop=False, skip_group_check=True)
                    rows = slice(64 * p, 64 * p + STK)
                    for q in (1, 0):
                        mm = pe.matmul(halves(bk)[:, 1 - q, :], q_stack[rows, g, q * P:(q + 1) * P],
                                       k_stack[rows, g, :], start=False, stop=(q == 0), skip_group_check=True)
                mm.then_inc(s_ps, 1)

            def transpose_max(a):
                pe.wait_ge(m_split, 2 * a + 2)
                for q in range(QT):
                    mm = pe.transpose(bank[0:32, 0, q * P:(q + 1) * P], mneg_s[:, q, :].bitcast(F32), ident[:])
                mm.then_inc(mT_ps, 1)

            def shifted(a, n):
                g, p = n // 2, n % 2
                if n == 0:
                    pe.wait_ge(shift_ld, 16 * 4 * (a + 1))
                if n < 2:
                    pe.wait_ge(mT_ok, a + 1)
                else:
                    pe.wait_ge(p_ok, H * a + n - 1)
                bk = n % 2
                pe.matmul(bank[:, bk, P:3 * P], ident_bf[:], causal_kq[:].rearrange("p a n -> p (a n)"),
                          start=True, stop=False, skip_group_check=True)
                rows = slice(64 * p, 64 * p + SX)
                for k in (1, 0):
                    mm = pe.matmul(halves(bk)[:, 1 - k, :], k_stack[rows, g, k * P:(k + 1) * P],
                                   q_stack[rows, g, :], start=False, stop=(k == 0), skip_group_check=True)
                mm.then_inc(st_ps, 1)

            def weigh(a, g):
                pe.wait_ge(p_ok, H * a + 4 * g + 4)
                if g == 0:
                    pe.wait_ge(v_ok, a + 1)
                dst = halves(2 + g // 2)[:, g % 2, :]
                for j in range(4):
                    pe.matmul(dst[32 * j:32 * j + 32, :], v_aug[:, 0, 4 * g + j, :],
                              probs[:, (4 * g + j) % 8, P:3 * P], start=True, stop=False, skip_group_check=True)
                for j in range(4):
                    mm = pe.matmul(dst[32 * j:32 * j + 32, P:T], v_aug[:, 1, 4 * g + j, :],
                                   probs[:, (4 * g + j) % 8, 0:P], start=False, stop=True, skip_group_check=True)
                mm.then_inc(pv_ps, 1)

            def turn_a(a):
                pe.wait_ge(u_ok, 2 * a + 2)
                for q in range(QT):
                    for g in range(4):
                        mm = pe.transpose(bank[:, q, g * P:(g + 1) * P], unnorm[:, g, q * P:(q + 1) * P], ident[:])
                mm.then_inc(ut_ps, 1)

            def turn_back_a(a):
                pe.wait_ge(att_ok, a + 1)
                for k in range(KD):
                    for q in range(QT):
                        mm = pe.transpose(bank[:, 2, k * T + q * P:k * T + (q + 1) * P],
                                          attn[:, q, k * P:(k + 1) * P], ident[:])
                mm.then_inc(atT_ps, 1)

            def output_a(a):
                pe.wait_ge(att_hi, a + 1)
                pe.wait_ge(att_lo, a + 1)
                for q in range(QT):
                    for k in range(KD):
                        mm = product(halves(0)[:, q, :], both(attn_s, slice(None), k, slice(q * P, (q + 1) * P)),
                                     both(wo, slice(None), k), k == 0, k == KD - 1)
                mm.then_inc(o_ps, 1)

            def transpose_b(b, n):
                pe.wait_ge(xn_b_ok, 2 * b + n + 1)
                pe.wait_ge(c2_lo, 4 * b + 4 * n)
                for k in range(KD):
                    for q in range(QT):
                        mm = pe.transpose(bank[:, 6, k * T + q * P:k * T + (q + 1) * P],
                                          xn_b[:, q, k * P:(k + 1) * P], ident[:])
                mm.then_inc(xbT_ps, 1)

            def queries(b, g):
                if g == 0:
                    pe.wait_ge(xbT_hi, 2 * b + 1)
                    pe.wait_ge(xbT_lo, 2 * b + 1)
                if g < 2:
                    pe.wait_ge(gl_ok, 4 * b)
                else:
                    pe.wait_ge(q2_lo, 4 * b + g - 1)
                for c in range(2):
                    m = 2 * g + c
                    for k in range(KD):
                        mm = product(halves(4 + g % 2)[:, c, :], both(wq2, slice(None), k, slice(m * P, (m + 1) * P)),
                                     both(xbT, slice(None), k), k == 0, k == KD - 1)
                mm.then_inc(q2_ps, 1)

            def scores2(b, g):
                if g == 0:
                    pe.wait_ge(q2_lo, 4 * b + 4)
                    pe.wait_ge(mask_ok, b + 1)
                    pe.wait_ge(k2_ld, 16 * 4 * (b + 1))
                else:
                    pe.wait_ge(p2T_ok, 4 * b + g)
                for c in range(2):
                    m = 2 * g + c
                    dst = halves(4 + c)
                    for q in range(QT):
                        pe.matmul(dst[:, q, 0:PAIR], ident_bf[:], mask_bf[:, q].rearrange("p a s -> p (a s)"),
                                  start=(q == 0), stop=False, skip_group_check=True)
                    for q in range(QT):
                        mm = product(dst[:, q, :], both(q2, slice(None), m, slice(q * P, (q + 1) * P)),
                                     both(k2, slice(None), slice(m * PAIR, m * PAIR + W)), False, q == QT - 1,
                                     skip_group_check=True)
                mm.then_inc(s2_ps, 1)

            def transpose2(b, g):
                pe.wait_ge(nrm_ok, 4 * b + g + 1)
                for c in range(2):
                    for p in range(2):
                        for q in range(QT):
                            mm = pe.transpose(bank[0:S2, 4 + c, p * T + q * P:p * T + (q + 1) * P],
                                              sc2[g % 2][:, c * QT + q, p, :], ident[:])
                mm.then_inc(t2_ps, 1)

            def weigh2(b, g):
                pe.wait_ge(p2T_ok, 4 * b + g + 1)
                if g == 0:
                    pe.wait_ge(v2_ld, 16 * (b + 1))
                    pe.wait_ge(xbT_lo, 2 * b + 1)
                else:
                    pe.wait_ge(c2_lo, 4 * b + g)
                for c in range(2):
                    for j in range(4):
                        col = (2 * g + c) * P + 32 * j
                        mm = pe.matmul(halves(6)[32 * j:32 * j + 32, c, :], v2[:, col:col + 32],
                                       p2T[:, 2 * c + j // 2, :], start=True, stop=True, skip_group_check=True)
                mm.then_inc(c2_ps, 1)

            def output2(b, g):
                pe.wait_ge(c2_hi, 4 * b + g + 1)
                pe.wait_ge(c2_lo, 4 * b + g + 1)
                if g == 0:
                    pe.wait_ge(y_ok, b)
                for c in range(2):
                    m = 2 * g + c
                    for q in range(QT):
                        mm = product(halves(7)[:, q, :], both(c2, slice(None), c, slice(q * P, (q + 1) * P)),
                                     both(wo2, slice(None), m), m == 0 and q == 0, m == XM - 1,
                                     skip_group_check=True)
                mm.then_inc(o2_ps, 1)

            def hidden(b, g):
                if g == 0:
                    pe.wait_ge(xbT_hi, 2 * b + 2)
                    pe.wait_ge(xbT_lo, 2 * b + 2)
                if g < 2:
                    pe.wait_ge(p2T_ok, 4 * b + 4)
                else:
                    pe.wait_ge(gl_ok, 4 * b + g - 1)
                for c in range(2):
                    m = 2 * g + c
                    for k in range(KD):
                        mm = product(halves(4 + g % 2)[:, c, :], both(wfc, slice(None), k, slice(m * P, (m + 1) * P)),
                                     both(xbT, slice(None), k), k == 0, k == KD - 1)
                mm.then_inc(fc_ps, 1)

            def project_down(b, g):
                if g == 0:
                    pe.wait_ge(x2_ok, b + 1)
                pe.wait_ge(hid_lo, 4 * b + g + 1)
                for c in range(2):
                    m = 2 * g + c
                    for q in range(QT):
                        mm = product(halves(7)[:, q, :], both(hid, slice(None), m, slice(q * P, (q + 1) * P)),
                                     both(wpj, slice(None), m), m == 0 and q == 0, m == FM - 1,
                                     skip_group_check=True)
                if g == 3:
                    mm.then_inc(y_ps, 1)

            def step(a, b):
                A, B = a is not None, b is not None
                if A:
                    transpose_a(a)
                if B:
                    transpose_b(b, 0)
                if A:
                    project(a)
                if B:
                    for g in range(4):
                        queries(b, g)
                    scores2(b, 0)
                if A:
                    scores(a, 0)
                    scores(a, 1)
                if B:
                    transpose2(b, 0)
                if A:
                    scores(a, 2)
                    scores(a, 3)
                if B:
                    weigh2(b, 0)
                    scores2(b, 1)
                if A:
                    scores(a, 4)
                    scores(a, 5)
                if B:
                    output2(b, 0)
                    transpose2(b, 1)
                if A:
                    scores(a, 6)
                    scores(a, 7)
                if B:
                    weigh2(b, 1)
                    scores2(b, 2)
                if A:
                    transpose_max(a)
                if B:
                    output2(b, 1)
                    transpose2(b, 2)
                    weigh2(b, 2)
                    scores2(b, 3)
                    output2(b, 2)
                if A:
                    for n in range(4):
                        shifted(a, n)
                if B:
                    transpose2(b, 3)
                if A:
                    for n in range(4, 8):
                        shifted(a, n)
                    weigh(a, 0)
                if B:
                    weigh2(b, 3)
                if A:
                    for n in range(8, 12):
                        shifted(a, n)
                    weigh(a, 1)
                if B:
                    output2(b, 3)
                if A:
                    for n in range(12, 16):
                        shifted(a, n)
                    weigh(a, 2)
                    weigh(a, 3)
                if B:
                    transpose_b(b, 1)
                    hidden(b, 0)
                if A:
                    turn_a(a)
                if B:
                    hidden(b, 1)
                    hidden(b, 2)
                if A:
                    turn_back_a(a)
                if B:
                    hidden(b, 3)
                if A:
                    output_a(a)
                if B:
                    for g in range(4):
                        project_down(b, g)

            pe.wait_ge(const_ok, 8)
            pe.wait_ge(w_lo, WO_W + 1)
            start_b()
            elements(step)(pe)

        @block.scalar
        def _(act):
            def split_hi(k):
                act.wait_ge(raw_ld[k % 2], raw_count[k])
                if k == WV_W:
                    act.wait_ge(kx_ps, 2 * XM)
                if k == FC_W:
                    act.wait_ge(wstep, 6)
                if k == PJ_W:
                    act.wait_ge(wstep, 12)
                act.activation(split_to[k][0], raw_of[k], ACT.Copy).then_inc(w_hi, 1)

            def start_b():
                split_hi(WK_W)
                split_hi(CTX_W)
                for n in range(2 * XM):
                    act.wait_ge(kx_ps, n + 1)
                    if n >= 2:
                        act.wait_ge(kx_st[n % 2], 32 * (n // 2))
                    act.activation(k_out[n % 2][0], bank[:, 4 + n % 4, 0:HS], ACT.Copy).then_inc(kx_hi, 1)
                split_hi(WV_W)
                split_hi(WQ_W)
                for n in range(2 * NB):
                    act.wait_ge(vx_ps, n + 1)
                    if n >= 2:
                        act.wait_ge(vx_st[n % 2], 16 * (n // 2))
                    act.activation(v2[:, (n % 2) * 512:(n % 2 + 1) * 512], bank[0:S2, 4 + n % 4, :],
                                   ACT.Copy).then_inc(vx_ok, 1)
                split_hi(WO2_W)
                split_hi(FC_W)
                split_hi(PJ_W)

            def copy(dst, src, done):
                act.activation(dst, src, ACT.Copy).then_inc(done, 1)

            def xaT_part(a):
                act.wait_ge(xaT_ps, a + 1)
                act.wait_ge(v_ps, a)
                copy(xaT[0][:].rearrange("p k t -> p (k t)"), bank[:, 0, :], xaT_hi)

            def values(a):
                act.wait_ge(v_ps, a + 1)
                act.wait_ge(pv_ps, 4 * a)
                copy(v_aug[:, :, :, 0:DH], halves(3).rearrange("p q (h d) -> p q h d", h=H), v_ok)

            def rotated(a, w):
                act.wait_ge(rot_ok, 2 * a + w + 1)
                if w == 0:
                    act.wait_ge(o_ps, a)
                copy(rot_s[0][:, w], rot[:, w], rot_hi)

            def maxima(a):
                act.wait_ge(mT_ps, a + 1)
                act.wait_ge(shift_ld, 64 * a)
                copy(mnegT[:], bank[0:32, 0, 0:T], mT_ok)

            def exponentials(a, n):
                act.wait_ge(st_ps, H * a + n + 1)
                if n < 8:
                    if n == 0:
                        act.wait_ge(pv_ps, 4 * a)
                        act.wait_ge(rot_ok, 2 * a + 2)
                else:
                    act.wait_ge(pv_ps, 4 * a + n // 4 - 1)
                act.activation(probs[:, n % 8, :], bank[:, n % 2, P:4 * P], ACT.Exp, scale=SCALE).then_inc(p_ok, 1)

            def unnormalised(a, c):
                act.wait_ge(pv_ps, 4 * a + 2 * c + 2)
                if c == 0:
                    act.wait_ge(rot_lo, 2 * a + 2)
                copy(unnorm[:, 2 * c:2 * c + 2], halves(2 + c), u_ok)

            def attention_hi(a):
                act.wait_ge(atT_ps, a + 1)
                act.wait_ge(stack_ld, 16 * 24 * (a + 1))
                copy(attn_s[0].rearrange("p k t -> p (k t)"), bank[:, 2, :], att_hi)

            def xbT_part(b, n):
                act.wait_ge(xbT_ps, 2 * b + n + 1)
                act.wait_ge(fc_ps if n == 0 else q2_ps, 4 * b + 4 * n)
                copy(xbT[0][:].rearrange("p k t -> p (k t)"), bank[:, 6, :], xbT_hi)

            def queries(b, g):
                act.wait_ge(q2_ps, 4 * b + g + 1)
                if g == 0:
                    act.wait_ge(y_ps, b)
                copy(q2[0][:, 2 * g:2 * g + 2], halves(4 + g % 2), q2_hi)

            def exponentials2(b, g):
                act.wait_ge(sub_ok, 4 * b + g + 1)
                act.activation(sc2[g % 2], sc2[g % 2], ACT.Exp, scale=XSCALE).then_inc(e2_ok, 1)

            def probabilities2(b, g):
                act.wait_ge(t2_ps, 4 * b + g + 1)
                if g == 0:
                    act.wait_ge(hid_lo, 4 * b)
                else:
                    act.wait_ge(c2_ps, 4 * b + g)
                copy(p2T.rearrange("p (c a) t -> p c (a t)", c=2), bank[0:S2, 4:6, :], p2T_ok)

            def context_hi(b, g):
                act.wait_ge(c2_ps, 4 * b + g + 1)
                act.wait_ge(o2_ps, 4 * b + g)
                copy(c2[0][:], halves(6), c2_hi)

            def hidden(b, g):
                act.wait_ge(fc_ps, 4 * b + g + 1)
                if g == 0:
                    act.wait_ge(c2_ps, 4 * b + 4)
                    act.wait_ge(s2_ps, 4 * b + 4)
                if g >= 2:
                    act.wait_ge(hid_lo, 4 * b + g - 1)
                for c in range(2):
                    m = 2 * g + c
                    last = act.activation(gl[:, g % 2, c, :], halves(4 + g % 2)[:, c, :], ACT.Gelu,
                                          bias=bfc_t[:, m:m + 1])
                last.then_inc(gl_ok, 1)
                act.wait_ge(gl_ok, 4 * b + g + 1)
                copy(hid[0][:, 2 * g:2 * g + 2], gl[:, g % 2], hid_hi)

            def step(a, b):
                A, B = a is not None, b is not None
                if A:
                    xaT_part(a)
                if B:
                    xbT_part(b, 0)
                if A:
                    rotated(a, 0)
                    rotated(a, 1)
                    values(a)
                if B:
                    for g in range(4):
                        queries(b, g)
                    exponentials2(b, 0)
                    probabilities2(b, 0)
                    context_hi(b, 0)
                    exponentials2(b, 1)
                    probabilities2(b, 1)
                    context_hi(b, 1)
                    exponentials2(b, 2)
                if A:
                    maxima(a)
                if B:
                    probabilities2(b, 2)
                    context_hi(b, 2)
                    exponentials2(b, 3)
                if A:
                    for n in range(4):
                        exponentials(a, n)
                if B:
                    probabilities2(b, 3)
                if A:
                    for n in range(4, 8):
                        exponentials(a, n)
                if B:
                    context_hi(b, 3)
                if A:
                    for n in range(8, 12):
                        exponentials(a, n)
                    unnormalised(a, 0)
                    for n in range(12, 16):
                        exponentials(a, n)
                    unnormalised(a, 1)
                if B:
                    xbT_part(b, 1)
                    hidden(b, 0)
                    hidden(b, 1)
                    hidden(b, 2)
                if A:
                    attention_hi(a)
                if B:
                    hidden(b, 3)

            act.wait_ge(const_ld, 16 * 4)
            split_hi(QKV_W)
            split_hi(WO_W)
            start_b()
            elements(step)(act)

        @block.vector
        def _(dve):
            def split_lo(k):
                dve.wait_ge(w_hi, k + 1)
                dve.tensor_tensor(split_to[k][1], raw_of[k], split_to[k][0].bitcast(F32),
                                  ALU.subtract).then_inc(w_lo, 1)

            def quantise(n, k):
                w = raw_of[k]
                dve.wait_ge(raw_ld[k % 2], raw_count[k])
                dve.tensor_reduce(wmax[:, 0:1], w, AX_X, ALU.max, apply_absolute_value=True).then_inc(wmax_ok, 1)
                dve.wait_ge(wmax_all, n + 1)
                dve.tensor_scalar(wscale[:, n:n + 1], wmax[:, 1:2], 1.0 / QMAX, None, ALU.mult).then_inc(wstep, 1)
                dve.wait_ge(wstep, 6 * n + 1)
                dve.reciprocal(winv[:, n:n + 1], wscale[:, n:n + 1]).then_inc(wstep, 1)
                dve.wait_ge(wstep, 6 * n + 2)
                dve.tensor_scalar(w, w, winv[:, n:n + 1], ROUND, ALU.mult, ALU.add).then_inc(wstep, 1)
                dve.wait_ge(wstep, 6 * n + 3)
                dve.tensor_scalar(w, w, ROUND, QMAX, ALU.subtract, ALU.min).then_inc(wstep, 1)
                dve.wait_ge(wstep, 6 * n + 4)
                dve.tensor_scalar(w, w, -QMAX - 1.0, wscale[:, n:n + 1], ALU.max, ALU.mult).then_inc(wstep, 1)
                dve.wait_ge(wstep, 6 * n + 5)
                dve.wait_ge(lora_ps, n + 1)
                dve.scalar_tensor_tensor(out=w, in0=bank[:, 4:8, :].rearrange("p b n -> p (b n)"), scalar=LORA_SCALE,
                                         in1=w, op0=ALU.mult, op1=ALU.add).then_inc(wstep, 1)

            def start_b():
                split_lo(WK_W)
                split_lo(CTX_W)
                for n in range(2 * XM):
                    dve.wait_ge(kx_hi, n + 1)
                    dve.tensor_tensor(k_out[n % 2][1], bank[:, 4 + n % 4, 0:HS], k_out[n % 2][0].bitcast(F32),
                                      ALU.subtract).then_inc(kx_lo, 1)
                split_lo(WV_W)
                split_lo(WQ_W)
                split_lo(WO2_W)
                quantise(0, FC_W)
                split_lo(FC_W)
                quantise(1, PJ_W)
                split_lo(PJ_W)

            def norm(src, xn, st, mv, rs, sems, ve_ok, n, free):
                st_ok, mv_ok, rs_ok, xn_ok = sems
                for q in range(QT):
                    last = dve.bn_stats(st[:, q, :], src[:, q, :])
                last.then_inc(st_ok, 1)
                dve.wait_ge(st_ok, n + 1)
                dve.sem_inc(waited_dve, 1)
                for q in range(QT):
                    last = dve.bn_aggr(mv[:, q, :], st[:, q, :])
                last.then_inc(mv_ok, 1)
                dve.wait_ge(mv_ok, n + 1)
                dve.tensor_scalar(rs[:], mv[:, :, 1:2], EPS, None, ALU.add).then_inc(ve_ok, 1)
                dve.wait_ge(rs_ok, n + 1)
                free()
                for q in range(QT):
                    last = dve.tensor_scalar(xn[:, q, :], src[:, q, :], mv[:, q, 0:1], rs[:, q, :],
                                             ALU.subtract, ALU.mult)
                last.then_inc(xn_ok, 1)

            def low(dst, src, hi, done):
                dve.tensor_tensor(dst, src, hi.bitcast(F32), ALU.subtract).then_inc(done, 1)

            def norm_a(a):
                dve.wait_ge(x_ld, 16 * (a + 1))
                norm(x_in, xn_a, st_a, mv_a, rs_a, (lna_st, lna_mv, lna_rs, xn_a_ok), lna_ve, a,
                     lambda: dve.wait_ge(xaT_ps, a))
                dve.wait_ge(xaT_hi, a + 1)
                low(xaT[1][:].rearrange("p k t -> p (k t)"), bank[:, 0, :],
                    xaT[0][:].rearrange("p k t -> p (k t)"), xaT_lo)

            def rotary(a, w):
                dve.wait_ge(qk_ps, 2 * a + w + 1)
                if w == 0:
                    dve.wait_ge(pv_ps, 4 * a)
                else:
                    dve.wait_ge(rot_ok, 2 * a + w)
                for dst, table in ((tcos, cos_t), (tsin, sin_t)):
                    last = dve.tensor_tensor(dst, halves(1 + w),
                                             table[:].rearrange("p t -> p () t").broadcast_to([P, 2, T]), ALU.mult)
                last.then_inc(trig, 1)

            def maxima(a, g):
                dve.wait_ge(s_ps, 8 * a + g + 1)
                if g == 0:
                    dve.wait_ge(m_split, 2 * a)
                b0 = 2 * (g % 2)
                for q in range(QT):
                    n = (q + 1) * P
                    off = (1 - q) * W
                    last = dve.tensor_reduce(mneg[:, q, :, g:g + 1], bank[:, b0:b0 + 2, off:off + n], AX_X, ALU.max,
                                             negate=True)
                last.then_inc(s_max, 1)

            def split_max(a):
                dve.wait_ge(s_max, 8 * a + 8)
                dve.wait_ge(mT_ps, a)
                m = mneg[:].rearrange("p q a h -> p q (a h)")
                dve.tensor_copy(mneg_s[:, :, 0:H], m).then_inc(m_split, 1)
                dve.wait_ge(m_split, 2 * a + 1)
                low(mneg_s[:, :, H:2 * H], m, mneg_s[:, :, 0:H], m_split)

            def attention(a):
                dve.wait_ge(ut_ps, a + 1)
                u = bank[:, 0:QT, :].rearrange("p q (h e) -> p q h e", h=H)
                dve.reciprocal(rc_a[:], u[:, :, :, DH]).then_inc(rca_ok, 1)
                dve.wait_ge(rca_ok, a + 1)
                for q in range(QT):
                    last = dve.tensor_tensor(attn[:, q, :].rearrange("p (h d) -> p h d", h=H), u[:, q, :, 0:DH],
                                             rc_a[:, q].rearrange("p h -> p h ()").broadcast_to([P, H, DH]), ALU.mult)
                last.then_inc(att_ok, 1)

            def attention_lo(a):
                dve.wait_ge(att_hi, a + 1)
                low(attn_s[1].rearrange("p k t -> p (k t)"), bank[:, 2, :],
                    attn_s[0].rearrange("p k t -> p (k t)"), att_lo)

            def residual_a(a):
                dve.wait_ge(o_ps, a + 1)
                dve.wait_ge(xres_ld, 16 * (a + 1))
                dve.wait_ge(x2_ok, a)
                dve.tensor_tensor(x1[:], halves(0), x_res[:], ALU.add).then_inc(x1_ok, 1)

            def mask_bias(b):
                dve.wait_ge(mask_ld, 16 * (b + 1))
                dve.wait_ge(s2_ps, 4 * b)
                for q in range(QT):
                    last = dve.tensor_scalar(mask_bf[:, q], mask_u8[:, q:q + 1, :].broadcast_to([P, 2, S2]),
                                             NEG, None, ALU.mult)
                last.then_inc(mask_ok, 1)

            def norm_b(b, n):
                dve.wait_ge(x1_ok if n == 0 else x2_ok, b + 1)
                norm(x1 if n == 0 else x2, xn_b, st_b, mv_b, rs_b, (lnb_st, lnb_mv, lnb_rs, xn_b_ok), lnb_ve, 2 * b + n,
                     lambda: dve.wait_ge(xbT_ps, 2 * b + n))

            def xbT_part(b, n):
                dve.wait_ge(xbT_hi, 2 * b + n + 1)
                low(xbT[1][:].rearrange("p k t -> p (k t)"), bank[:, 6, :],
                    xbT[0][:].rearrange("p k t -> p (k t)"), xbT_lo)

            def queries(b, g):
                dve.wait_ge(q2_hi, 4 * b + g + 1)
                low(q2[1][:, 2 * g:2 * g + 2], halves(4 + g % 2), q2[0][:, 2 * g:2 * g + 2], q2_lo)

            def softmax2(b, g):
                r = g % 2
                dve.wait_ge(s2_ps, 4 * b + g + 1)
                ps = bank[:, 4:6, :].rearrange("p c (q n) -> p (c q) n", q=2)[:, :, 0:PAIR] \
                    .rearrange("p g (a s) -> p g a s", a=2)
                dve.tensor_reduce(mx2[:, r], ps, AX_X, ALU.max).then_inc(mx2_ok, 1)
                dve.wait_ge(mx2_ok, 4 * b + g + 1)
                if g < 2:
                    dve.wait_ge(t2_ps, 4 * b)
                else:
                    dve.wait_ge(t2_ps, 4 * b + g - 1)
                dve.tensor_tensor(sc2[r], ps, mx2[:, r].rearrange("p g a -> p g a ()").broadcast_to([P, 4, 2, S2]),
                                  ALU.subtract).then_inc(sub_ok, 1)

            def sums2(b, g):
                r = g % 2
                dve.wait_ge(e2_ok, 4 * b + g + 1)
                dve.tensor_reduce(sm2[:, r], sc2[r], AX_X, ALU.add).then_inc(sm2_ok, 1)
                dve.wait_ge(sm2_ok, 4 * b + g + 1)
                dve.reciprocal(rc2[:, r], sm2[:, r]).then_inc(rc2_ok, 1)

            def context_lo(b, g):
                dve.wait_ge(c2_hi, 4 * b + g + 1)
                low(c2[1][:], halves(6), c2[0][:], c2_lo)

            def residual_b(b):
                dve.wait_ge(o2_ps, 4 * b + 4)
                dve.wait_ge(x2b_ok, b)
                dve.tensor_tensor(x2[:], halves(7), x1[:], ALU.add).then_inc(x2_ok, 1)

            def result(b):
                dve.wait_ge(y_ps, b + 1)
                dve.wait_ge(x2b_ok, b + 1)
                dve.wait_ge(y_st, 16 * b)
                dve.tensor_tensor(y, halves(7), x2b, ALU.add).then_inc(y_ok, 1)

            def step(a, b):
                A, B = a is not None, b is not None
                if A:
                    norm_a(a)
                if B:
                    norm_b(b, 0)
                    xbT_part(b, 0)
                if A:
                    rotary(a, 0)
                    rotary(a, 1)
                if B:
                    mask_bias(b)
                    for g in range(4):
                        queries(b, g)
                    softmax2(b, 0)
                    sums2(b, 0)
                if A:
                    maxima(a, 0)
                    maxima(a, 1)
                    maxima(a, 2)
                    maxima(a, 3)
                if B:
                    context_lo(b, 0)
                    softmax2(b, 1)
                    sums2(b, 1)
                if A:
                    maxima(a, 4)
                    maxima(a, 5)
                    maxima(a, 6)
                    maxima(a, 7)
                    split_max(a)
                if B:
                    context_lo(b, 1)
                    softmax2(b, 2)
                    sums2(b, 2)
                    context_lo(b, 2)
                    softmax2(b, 3)
                    sums2(b, 3)
                    context_lo(b, 3)
                    residual_b(b)
                    norm_b(b, 1)
                    xbT_part(b, 1)
                if A:
                    attention(a)
                    attention_lo(a)
                    residual_a(a)
                if B:
                    result(b)

            dve.wait_ge(const_ld, 16 * 4)
            split_lo(QKV_W)
            split_lo(WO_W)
            start_b()
            elements(step)(dve)


IN_ORDER = ["x", "ctxT", "mask", "wqT", "wkT", "wvT", "woT", "wQ", "wK", "wV", "wO", "wfcT", "bfc", "Afc", "BfcT",
            "wpjT", "bpj", "Apj", "BpjT", "cos", "sin"]


def rotary_tables(tokens, head_width, repeat):
    half = head_width // 2
    theta = np.float32(10000.0) ** (np.float32(-2.0) * np.arange(half, dtype=np.float32) / np.float32(head_width))
    angles = np.arange(tokens, dtype=np.float32)[None, :] * theta.astype(np.float32)[:, None]
    rows = [np.tile(np.repeat(f(angles).astype(np.float32), repeat, axis=0), (2, 1)) for f in (np.cos, np.sin)]
    return rows


def kernel(x, ctx_1024, mask_BxSxS2_bk1, L0_attn_W_q, L0_attn_W_k, L0_attn_W_v, L0_attn_W_o, L0_xattn_W_Q,
           L0_xattn_W_K, L0_xattn_W_V, L0_xattn_W_O, L0_ffn_W_fc, L0_ffn_b_fc, L0_ffn_A_fc, L0_ffn_B_fc,
           L0_ffn_W_proj, L0_ffn_b_proj, L0_ffn_A_proj, L0_ffn_B_proj):
    import concourse.bacc as bacc
    from concourse.bass_utils import run_bass_kernel_spmd

    H = 16
    nb, tokens, d = x.shape
    hw = d // H

    def rotary_order(w):
        w = np.asarray(w).reshape(H // 2, 2, hw // 2, 2, d)
        return w.transpose(4, 3, 1, 2, 0).reshape(d, d)

    cos, sin = rotary_tables(tokens, hw, H // 2)
    f = L0_ffn_W_fc.shape[0]
    laid = {
        "x": x, "ctxT": np.asarray(ctx_1024).transpose(2, 0, 1).reshape(d, -1),
        "mask": np.asarray(mask_BxSxS2_bk1),
        "wqT": rotary_order(L0_attn_W_q), "wkT": rotary_order(L0_attn_W_k),
        "wvT": np.asarray(L0_attn_W_v).T, "woT": np.asarray(L0_attn_W_o).T,
        "wQ": L0_xattn_W_Q, "wK": L0_xattn_W_K, "wV": L0_xattn_W_V, "wO": L0_xattn_W_O,
        "wfcT": np.asarray(L0_ffn_W_fc).T, "bfc": np.asarray(L0_ffn_b_fc).reshape(f // P, P).T,
        "Afc": L0_ffn_A_fc, "BfcT": np.asarray(L0_ffn_B_fc).T,
        "wpjT": np.asarray(L0_ffn_W_proj).T, "bpj": np.asarray(L0_ffn_b_proj).reshape(1, d),
        "Apj": L0_ffn_A_proj, "BpjT": np.asarray(L0_ffn_B_proj).T, "cos": cos, "sin": sin,
    }
    nc = bacc.Bacc("TRN2", target_bir_lowering=False, num_devices=1)
    arrays, args = {}, []
    for name in IN_ORDER:
        a = np.ascontiguousarray(laid[name])
        arrays[f"in_{name}"] = a
        args.append(nc.dram_tensor(f"in_{name}", a.shape, mybir.dt.from_np(a.dtype), kind="ExternalInput").ap())
    out = nc.dram_tensor("out_y", x.shape, F32, kind="ExternalOutput").ap()
    decoder_layer(nc, *args, out)
    r = run_bass_kernel_spmd(nc, [arrays], core_ids=[0])
    return r.results[0]["out_y"]
```

```python
from contextlib import ExitStack

import numpy as np

import concourse.bass as bass
from concourse import mybir

P = 128
F32 = mybir.dt.float32
F32R = mybir.dt.float32r
BF16 = mybir.dt.bfloat16
U8 = mybir.dt.uint8
ALU = mybir.AluOpType
ACT = mybir.ActivationFunctionType
AX_X = mybir.AxisListType.X
RMAX = bass.bass_isa.ReduceOp.max

EPS = 1e-5
QMAX = 127.0
ROUND = 12582912.0
NEG = -float(2.0 ** 100)
LORA_SCALE = 2.0


def decoder_layer(nc, x, ctxT, mask, wqT, wkT, wvT, woT, wQ, wK, wV, wO, wfcT, bfc, Afc, BfcT,
                  wpjT, bpj, Apj, BpjT, cos, sin, out):
    NB, T, D = x.shape
    QT = T // P
    KD = D // P
    H = 16
    DH = D // H
    HH = H // 2
    HI = DH // 2
    S2 = mask.shape[2]
    XD = wQ.shape[1]
    XM = XD // P
    DX = XD // H
    R = Afc.shape[0]
    F = wfcT.shape[1]
    FM = F // P
    PAIR = 2 * S2
    W = 256
    STK = 3 * DH
    SX = STK + 2
    SCALE = float(DH) ** -0.5
    XSCALE = float(DX) ** -0.5

    with ExitStack() as ctx:
        def sb(name, shape, dt=F32):
            return ctx.enter_context(nc.sbuf_tensor(name, shape, dt))

        def sem(name):
            return ctx.enter_context(nc.semaphore(name))

        bank = ctx.enter_context(nc.psum_tensor("banks", [P, 8, 512], F32))

        def halves(b, w=W):
            return bank[:, b, :].rearrange("p (a n) -> p a n", n=w)

        ident = sb("ident", [P, P])
        ident_bf = sb("ident_bf", [P, P], BF16)
        causal_qk = sb("causal_qk", [P, 2, P], BF16)
        causal_kq = sb("causal_kq", [P, 2, P], BF16)
        cos_t = sb("cos_t", [P, T])
        sin_t = sb("sin_t", [P, T])
        bfc_t = sb("bfc_t", [P, FM])
        bpj_t = sb("bpj_t", [P, D])

        def pair(name, shape):
            return sb(name + "_hi", shape, F32R), sb(name + "_lo", shape, F32R)

        wqkv = pair("wqkv", [P, KD, 3 * D])
        wo = pair("wo", [P, KD, D])
        wq2 = pair("wq2", [P, KD, XD])
        wo2 = pair("wo2", [P, XM, D])
        wfc = pair("wfc", [P, KD, F])
        wpj = pair("wpj", [P, FM, D])

        x_in = sb("x_in", [P, QT, D])
        x_res = sb("x_res", [P, QT, D])
        xn_a = sb("xn_a", [P, QT, D])
        st_a = sb("st_a", [P, QT, 6])
        mv_a = sb("mv_a", [P, QT, 2])
        rs_a = sb("rs_a", [P, QT, 1])
        half_a = sb("half_a", [P, QT, 1])
        xaT = pair("xaT", [P, KD, T])
        rot = sb("rot", [P, 2, 2, T])
        rot_s = pair("rot_s", [P, 2, 2, T])
        unnorm = rot[:].rearrange("p a b t -> p (a b) t")
        attn = sb("attn", [P, QT, D])
        attn_s = [v[:] for v in pair("attn", [P, KD, T])]
        rc_a = sb("rc_a", [P, QT, H])
        q_stack = sb("q_stack", [P, HH, T], F32R)
        k_stack = sb("k_stack", [P, HH, T], F32R)
        v_aug = sb("v_aug", [P, QT, H, 32])
        probs = sb("probs", [P, 8, 3 * P])
        tcos = probs[:, 0:4, :].rearrange("p a b -> p (a b)")[:, 0:2 * T].rearrange("p (j t) -> p j t", j=2)
        tsin = probs[:, 4:8, :].rearrange("p a b -> p (a b)")[:, 0:2 * T].rearrange("p (j t) -> p j t", j=2)
        mneg = sb("mneg", [P, QT, 2, HH])
        mneg_s = sb("mneg_s", [P, QT, 2, 2, HH], F32R)
        mnegT = sb("mnegT", [32, T], F32R)
        x1 = sb("x1", [P, QT, D])

        x2 = sb("x2", [P, QT, D])
        st_b = sb("st_b", [P, QT, 6])
        mv_b = sb("mv_b", [P, QT, 2])
        rs_b = sb("rs_b", [P, QT, 1])
        xbT = pair("xbT", [P, KD, T])
        q2 = pair("q2", [P, XM, T])
        hid = q2
        KW = (XM - 1) * PAIR + W
        k2 = pair("k2", [P, KW])
        v2w = sb("v2", [P, XD])
        v2 = v2w[0:S2]
        mask_u8 = sb("mask_u8", [P, QT, S2], U8)
        mask_bf = sb("mask_bf", [P, QT, 2, S2], BF16)
        mx2 = sb("mx2", [P, 2, 4, 2])
        sm2 = sb("sm2", [P, 2, 4, 2])
        rc2 = sb("rc2", [P, 2, 4, 2])
        c2 = pair("c2", [P, 2, T])
        LOAD = KD * XD
        work = sb("work", [P, max(2 * LOAD, 4 * T + 16 * S2 + 3 * QT * D)])
        o = 4 * T
        p2T = work[0:S2, 0:o].rearrange("p (h t) -> p h t", t=T)
        gl = work[:, 0:o].rearrange("p (r a t) -> p r a t", r=2, t=T)
        sc2 = [work[:, o + r * 8 * S2:o + (r + 1) * 8 * S2].rearrange("p (g a s) -> p g a s", g=4, s=S2)
               for r in range(2)]
        o += 16 * S2
        x2b, xn_b, y = (work[:, o + j * QT * D:o + (j + 1) * QT * D].rearrange("p (q d) -> p q d", q=QT)
                        for j in range(3))

        NS = NB * S2
        HS = NS // 2
        VT = -(-NS // P)
        LOAD = KD * XD
        raw = [work[:, 0:LOAD], work[:, LOAD:2 * LOAD]]
        kv_w = [v[:].rearrange("p m t -> p (m t)").rearrange("p (k n) -> p k n", k=KD) for v in q2]
        ctx_s = [v[:, 0:KD * NS].rearrange("p (k n) -> p k n", k=KD) for v in k2]
        k_out = [[v[:].rearrange("p a t -> p (a t)")[:, 0:HS] for v in pr] for pr in (c2, xbT)]
        wmax = sb("wmax", [P, 2])
        wscale = sb("wscale", [P, 2])
        winv = sb("winv", [P, 2])

        k2_dram = nc.dram_tensor("k2_dram", [2, P, XM, NS], F32, kind="Internal").ap()
        v2_dram = nc.dram_tensor("v2_dram", [NS, XD], F32, kind="Internal").ap()

        block = ctx.enter_context(nc.Block())

        const_ld, const_ok, k2_zero = sem("const_ld"), sem("const_ok"), sem("k2_zero")
        raw_ld = [sem(f"raw{r}_ld") for r in range(2)] + [sem(f"raw{r}_reld") for r in range(2)]
        w_hi, w_lo = sem("w_hi"), sem("w_lo")
        kx_ps, kx_hi, kx_lo, kx_st = sem("kx_ps"), sem("kx_hi"), sem("kx_lo"), [sem(f"kx_st{r}") for r in range(2)]
        vx_ps, vx_ok, vx_st = sem("vx_ps"), sem("vx_ok"), [sem(f"vx_st{r}") for r in range(2)]
        lora_ld, lora_ps = sem("lora_ld"), sem("lora_ps")
        wmax_ok, wmax_all, wstep = sem("wmax_ok"), sem("wmax_all"), sem("wstep")
        waited_sp, waited_dve = sem("waited_sp"), sem("waited_dve")
        x_ld, xres_ld = sem("x_ld"), sem("xres_ld")
        lna_st, lna_mv, lna_rs, xn_a_ok = sem("lna_st"), sem("lna_mv"), sem("lna_rs"), sem("xn_a_ok")
        xaT_ps, xaT_hi, xaT_lo = sem("xaT_ps"), sem("xaT_hi"), sem("xaT_lo")
        qk_ps, v_ps, v_ok = sem("qk_ps"), sem("v_ps"), sem("v_ok")
        trig, rot_ok, rot_hi, rot_lo = sem("trig"), sem("rot_ok"), sem("rot_hi"), sem("rot_lo")
        stack_ld, shift_ld = sem("stack_ld"), sem("shift_ld")
        s_ps, s_max = sem("s_ps"), sem("s_max")
        m_split, mT_ps, mT_ok = sem("m_split"), sem("mT_ps"), sem("mT_ok")
        st_ps, p_ok, pv_ps = sem("st_ps"), sem("p_ok"), sem("pv_ps")
        u_ok, ut_ps, rca_ok, att_ok = sem("u_ok"), sem("ut_ps"), sem("rca_ok"), sem("att_ok")
        atT_ps, att_hi, att_lo = sem("atT_ps"), sem("att_hi"), sem("att_lo")
        lna_ve, lnb_ve = sem("lna_ve"), sem("lnb_ve")
        o_ps, x1_ok = sem("o_ps"), sem("x1_ok")
        lnb_st, lnb_mv, lnb_rs, xn_b_ok = sem("lnb_st"), sem("lnb_mv"), sem("lnb_rs"), sem("xn_b_ok")
        xbT_ps, xbT_hi, xbT_lo = sem("xbT_ps"), sem("xbT_hi"), sem("xbT_lo")
        mask_ld, mask_ok, k2_ld, v2_ld = sem("mask_ld"), sem("mask_ok"), sem("k2_ld"), sem("v2_ld")
        q2_ps, q2_hi, q2_lo = sem("q2_ps"), sem("q2_hi"), sem("q2_lo")
        s2_ps, mx2_ok, sub_ok, e2_ok = sem("s2_ps"), sem("mx2_ok"), sem("sub_ok"), sem("e2_ok")
        sm2_ok, rc2_ok, nrm_ok = sem("sm2_ok"), sem("rc2_ok"), sem("nrm_ok")
        t2_ps, p2T_ok, c2_ps, c2_hi, c2_lo = (sem(n) for n in ("t2_ps", "p2T_ok", "c2_ps", "c2_hi", "c2_lo"))
        o2_ps, x2_ok, x2b_ok = sem("o2_ps"), sem("x2_ok"), sem("x2b_ok")
        fc_ps, gl_ok, hid_hi, hid_lo = sem("fc_ps"), sem("gl_ok"), sem("hid_hi"), sem("hid_lo")
        y_ps, y_ok, y_st = sem("y_ps"), sem("y_ok"), sem("y_st")

        def elements(first, step):
            def run(eng):
                first()
                step(0, None, 1)
                step(1, 0, 2)
                with eng.Fori(2, NB - 1) as i:
                    step(i, i - 1, i + 1)
                step(NB - 1, NB - 2, None)
                step(None, NB - 1, None)
            return run

        N_CONST = 5
        QKV_W, WO_W, WK_W, CTX_W, WV_W, WQ_W, WO2_W, FC_W, PJ_W = range(9)
        split_to = [[v[:].rearrange("p k n -> p (k n)") for v in wqkv],
                    [v[:].rearrange("p k n -> p (k n)") for v in wo],
                    [v.rearrange("p k n -> p (k n)") for v in kv_w],
                    [v[:, 0:KD * NS] for v in k2],
                    [v.rearrange("p k n -> p (k n)") for v in kv_w]] + [
                    [v[:].rearrange("p k n -> p (k n)") for v in pr] for pr in (wq2, wo2, wfc, wpj)]
        raw_of = [raw[k % 2][:, 0:split_to[k][0].shape[1]] for k in range(9)]
        RAW_DMAS = [3, 1, 1, 1, 1, 1, 1, 1, 1]
        raw_sem = [raw_ld[k] if k < 2 else raw_ld[2 + k % 2] for k in range(9)]
        raw_count = [16 * RAW_DMAS[k] if k < 2 else 16 * (k // 2) for k in range(9)]

        def load_raw(eng, k, *views):
            if k >= 2:
                eng.wait_ge(w_lo, k - 1)
            for dst, src in views:
                eng.dma_start(dst, src).then_inc(raw_sem[k], 16)

        def tiles(k, n):
            return raw_of[k].rearrange("p (k n) -> p k n", n=n)

        def rows(w):
            return w.rearrange("(k p) n -> p k n", p=P)

        @block.sync
        def _(sp):
            sp.dma_start(x_in[:], x[0].rearrange("(q p) d -> p q d", p=P)).then_inc(x_ld, 16)
            load_raw(sp, QKV_W, *[(tiles(QKV_W, 3 * D)[:, :, j * D:(j + 1) * D], rows(w))
                              for j, w in enumerate((wqT, wkT, wvT))])
            sp.dma_start(cos_t[:], cos).then_inc(const_ld, 16)
            sp.dma_start(sin_t[:], sin).then_inc(const_ld, 16)
            sp.dma_start(bfc_t[:], bfc).then_inc(const_ld, 16)
            sp.dma_start(bpj_t[:], bpj.broadcast_to([P, D])).then_inc(const_ld, 16)
            load_raw(sp, WO_W, (tiles(WO_W, D), rows(woT)))

            def load_x(n):
                sp.wait_ge(xn_a_ok, n)
                sp.sem_inc(waited_sp, 1)
                sp.dma_start(x_in[:], x[n].rearrange("(q p) d -> p q d", p=P)).then_inc(x_ld, 16)

            def stacks(n):
                for w, (stack, order) in enumerate(((q_stack, (0, 0, 1)), (k_stack, (0, 1, 0)))):
                    if w == 0:
                        sp.wait_ge(st_ps, H * n)
                    for piece, done in ((0, rot_hi), (1, rot_lo)):
                        sp.wait_ge(done, 2 * n + w + 1)
                        for c in range(3):
                            if order[c] != piece:
                                continue
                            for p in range(2):
                                for j in range(2):
                                    row = 64 * p + c * DH + j * HI
                                    sp.dma_start(stack[row:row + HI, :, :].bitcast(F32),
                                                 rot_s[piece][64 * p:64 * p + 64, w, j, :].bitcast(F32)
                                                 ).then_inc(stack_ld, 16)

            def context(b):
                if isinstance(b, int) and b == 0:
                    for r in range(2):
                        sp.wait_ge(kx_st[r], 16 * 2 * XM)
                    sp.wait_ge(k2_zero, 1)
                sp.wait_ge(mask_ok, b)
                sp.sem_inc(waited_sp, 1)
                sp.dma_start(mask_u8[:], mask[b].rearrange("(q p) s -> p q s", p=P)).then_inc(mask_ld, 16)
                sp.wait_ge(s2_ps, 4 * b)
                sp.sem_inc(waited_sp, 1)
                for piece in range(2):
                    for p in range(2):
                        dst = k2[piece][64 * p:64 * p + DX, 0:XM * PAIR].bitcast(F32)
                        sp.dma_start(
                            dst.rearrange("p (m a s) -> p m a s", a=2, s=S2)[:, :, p, :],
                            k2_dram[piece, 64 * p:64 * p + DX].rearrange("p m (b s) -> p m b s", s=S2)[:, :, b, :]
                        ).then_inc(k2_ld, 16)

            def context_values(b):
                if isinstance(b, int) and b == 0:
                    for r in range(2):
                        sp.wait_ge(vx_st[r], 16 * VT)
                    sp.wait_ge(lora_ps, 2)
                sp.wait_ge(c2_ps, 4 * b)
                sp.sem_inc(waited_sp, 1)
                sp.dma_start(v2, v2_dram.rearrange("(b s) n -> b s n", s=S2)[b]).then_inc(v2_ld, 16)

            def first():
                stacks(0)

            def step(a, b, n):
                if a is not None:
                    sp.wait_ge(x1_ok, a)
                    sp.sem_inc(waited_sp, 1)
                    sp.dma_start(x_res[:], x[a].rearrange("(q p) d -> p q d", p=P)).then_inc(xres_ld, 16)
                    if n is not None:
                        load_x(n)
                    sp.wait_ge(mT_ok, a + 1)
                    for p in range(2):
                        sp.dma_start(q_stack[64 * p + STK:64 * p + SX, :, :].bitcast(F32),
                                     mnegT[p * H:(p + 1) * H, :].bitcast(F32)).then_inc(shift_ld, 16)
                    context(a)
                if n is not None:
                    stacks(n)
                if a is not None:
                    context_values(a)

            elements(first, step)(sp)

        @block.gpsimd
        def _(pool):
            pool.memset(ident[:], 0.0)
            pool.memset(causal_qk[:], 0.0)
            pool.memset(causal_kq[:], 0.0).then_inc(const_ok, 1)
            pool.wait_ge(const_ok, 1)
            pool.affine_select(out=ident[:], in_=ident[:], compare_op=ALU.not_equal, fill=1.0, base=0,
                               pattern=[[-1, P]], channel_multiplier=1).then_inc(const_ok, 1)
            pool.affine_select(out=causal_qk[:], in_=causal_qk[:], compare_op=ALU.is_ge, fill=NEG, base=0,
                               pattern=[[0, 2], [-1, P]], channel_multiplier=1).then_inc(const_ok, 1)
            pool.affine_select(out=causal_kq[:], in_=causal_kq[:], compare_op=ALU.is_ge, fill=NEG, base=0,
                               pattern=[[0, 2], [1, P]], channel_multiplier=-1).then_inc(const_ok, 1)
            pool.wait_ge(const_ok, 2)
            pool.tensor_copy(ident_bf[:], ident[:]).then_inc(const_ok, 1)
            pool.memset(half_a[:], -0.5)
            pool.memset(v_aug[:], 0.0).then_inc(const_ok, 1)
            pool.wait_ge(const_ok, 6)
            pool.memset(v_aug[:, :, :, DH:DH + 1], 1.0).then_inc(const_ok, 1)
            pool.memset(k_stack[:].bitcast(F32), 1.0).then_inc(const_ok, 1)

            def start_b():
                load_raw(pool, WK_W, (tiles(WK_W, XD), rows(wK)))
                load_raw(pool, CTX_W, (tiles(CTX_W, NS), rows(ctxT)))
                load_raw(pool, WV_W, (tiles(WV_W, XD), rows(wV)))
                for m in range(XM):
                    for half in range(2):
                        n = 2 * m + half
                        pool.wait_ge(kx_lo, n + 1)
                        for piece in range(2):
                            pool.dma_start(k2_dram[piece, :, m, half * HS:(half + 1) * HS],
                                           k_out[n % 2][piece].bitcast(F32)).then_inc(kx_st[n % 2], 16)
                load_raw(pool, WQ_W, (tiles(WQ_W, XD), rows(wQ)))
                for t in range(VT):
                    rows_t = min(P, NS - t * P)
                    for half in range(2):
                        n = 2 * t + half
                        pool.wait_ge(vx_ok, n + 1)
                        pool.dma_start(v2_dram[t * P:t * P + rows_t, half * 512:(half + 1) * 512],
                                       v2w[0:rows_t, half * 512:(half + 1) * 512]).then_inc(vx_st[n % 2], 16)
                for v in k2:
                    last = pool.memset(v[:].bitcast(F32), 0.0)
                last.then_inc(k2_zero, 1)
                load_raw(pool, WO2_W, (tiles(WO2_W, D), rows(wO)))
                load_raw(pool, FC_W, (tiles(FC_W, F), rows(wfcT)))
                pool.dma_start(x2[0:R, 0, :], Afc).then_inc(lora_ld, 16)
                pool.dma_start(x2[0:R, 1, :], BpjT).then_inc(lora_ld, 16)
                for r in range(2):
                    pool.wait_ge(vx_st[r], 16 * VT)
                pool.dma_start(v2[0:R, :], BfcT).then_inc(lora_ld, 16)
                load_raw(pool, PJ_W, (tiles(PJ_W, D), rows(wpjT)))

            def quantisers():
                for n in range(2):
                    if n == 1:
                        pool.wait_ge(lora_ps, 1)
                        pool.dma_start(v2[0:R, :], Apj).then_inc(lora_ld, 16)
                    pool.wait_ge(wmax_ok, n + 1)
                    pool.partition_all_reduce(wmax[:, 1:2], wmax[:, 0:1], P, RMAX).then_inc(wmax_all, 1)
                    pool.wait_ge(wstep, 6 * n + 1)

            def rotate(a, w):
                pool.wait_ge(trig, 2 * a + w + 1)
                if w == 0:
                    pool.wait_ge(ut_ps, a)
                pool.tensor_tensor(rot[:, w, 0, :], tcos[:, 0, :], tsin[:, 1, :], ALU.subtract)
                pool.tensor_tensor(rot[:, w, 1, :], tcos[:, 1, :], tsin[:, 0, :], ALU.add).then_inc(rot_ok, 1)
                pool.wait_ge(rot_hi, 2 * a + w + 1)
                pool.wait_ge(rot_ok, 2 * a + w + 1)
                pool.tensor_tensor(rot_s[1][:, w], rot[:, w], rot_s[0][:, w].bitcast(F32),
                                   ALU.subtract).then_inc(rot_lo, 1)

            def inverse_deviation(rs, ve_ok, rs_ok, n):
                pool.wait_ge(ve_ok, n + 1)
                pool.tensor_tensor(rs[:], rs[:], half_a[:], ALU.pow).then_inc(rs_ok, 1)

            def normalise(b, g):
                pool.wait_ge(rc2_ok, 4 * b + g + 1)
                pool.tensor_tensor(sc2[g % 2], sc2[g % 2],
                                   rc2[:, g % 2].rearrange("p g a -> p g a ()").broadcast_to([P, 4, 2, S2]),
                                   ALU.mult).then_inc(nrm_ok, 1)

            def residual_bias(b):
                pool.wait_ge(x2_ok, b + 1)
                pool.wait_ge(y_ok, b)
                for q in range(QT):
                    last = pool.tensor_tensor(x2b[:, q, :], x2[:, q, :], bpj_t[:], ALU.add)
                last.then_inc(x2b_ok, 1)

            def first():
                inverse_deviation(rs_a, lna_ve, lna_rs, 0)
                rotate(0, 0)
                rotate(0, 1)
                start_b()

            def step(a, b, n):
                A, B, N = a is not None, b is not None, n is not None
                if B:
                    normalise(b, 0)
                    normalise(b, 1)
                if N:
                    inverse_deviation(rs_a, lna_ve, lna_rs, n)
                if B:
                    normalise(b, 2)
                    normalise(b, 3)
                    inverse_deviation(rs_b, lnb_ve, lnb_rs, 2 * b + 1)
                    residual_bias(b)
                if N:
                    rotate(n, 0)
                    rotate(n, 1)
                if A and not B:
                    quantisers()
                if A:
                    inverse_deviation(rs_b, lnb_ve, lnb_rs, 2 * a)
                if B:
                    pool.wait_ge(y_ok, b + 1)
                    pool.dma_start(out[b].rearrange("(q p) d -> p q d", p=P), y).then_inc(y_st, 16)

            elements(first, step)(pool)
            pool.wait_ge(y_st, 16 * NB)

        @block.tensor
        def _(pe):
            def product(dst, w, x_, first, last, **kw):
                pe.matmul(dst, w[0], x_[0], start=first, stop=False, **kw)
                pe.matmul(dst, w[0], x_[1], start=False, stop=False, **kw)
                return pe.matmul(dst, w[1], x_[0], start=False, stop=last, **kw)

            def both(pr, *index):
                return [v[index] for v in pr]

            def keys(m):
                if m == 0:
                    pe.wait_ge(w_lo, CTX_W + 1)
                for half in range(2):
                    n = 2 * m + half
                    if n >= 4:
                        pe.wait_ge(kx_lo, n - 3)
                    for k in range(KD):
                        mm = product(bank[:, 3 + n % 4, 0:HS], both(kv_w, slice(None), k, slice(m * P, m * P + P)),
                                     both(ctx_s, slice(None), k, slice(half * HS, (half + 1) * HS)),
                                     k == 0, k == KD - 1)
                    mm.then_inc(kx_ps, 1)

            def values2(t):
                if t == 0:
                    pe.wait_ge(w_lo, WV_W + 1)
                    pe.wait_ge(kx_lo, 2 * XM)
                rows = min(P, NS - t * P)
                for half in range(2):
                    n = 2 * t + half
                    if n >= 4:
                        pe.wait_ge(vx_ok, n - 3)
                    for k in range(KD):
                        mm = product(bank[0:rows, 3 + n % 4, :], both(ctx_s, slice(None), k, slice(t * P, t * P + rows)),
                                     both(kv_w, slice(None), k, slice(half * 512, (half + 1) * 512)),
                                     k == 0, k == KD - 1)
                    mm.then_inc(vx_ps, 1)

            def lora_up():
                pe.wait_ge(vx_ok, 2 * VT)
                pe.wait_ge(lora_ld, 16 * 3)
                for k in range(KD):
                    for half in range(2):
                        mm = pe.matmul(bank[:, 3 + 2 * k + half, :], x2[0:R, 0, k * P:(k + 1) * P],
                                       v2[0:R, half * 512:(half + 1) * 512], start=True, stop=True)
                mm.then_inc(lora_ps, 1)

            def lora_down():
                pe.wait_ge(lora_ld, 16 * 4)
                pe.wait_ge(wstep, 6)
                for m in range(FM):
                    mm = pe.matmul(bank[:, 3 + m // 2, (m % 2) * D:(m % 2 + 1) * D], v2[0:R, m * P:(m + 1) * P],
                                   x2[0:R, 1, :], start=True, stop=True)
                mm.then_inc(lora_ps, 1)

            def transpose_a(a):
                pe.wait_ge(xn_a_ok, a + 1)
                for k in range(KD):
                    for q in range(QT):
                        mm = pe.transpose(bank[:, 2, k * T + q * P:k * T + (q + 1) * P],
                                          xn_a[:, q, k * P:(k + 1) * P], ident[:])
                mm.then_inc(xaT_ps, 1)

            def project(a, w):
                if w == 0:
                    pe.wait_ge(xaT_hi, a + 1)
                    pe.wait_ge(xaT_lo, a + 1)
                    pe.wait_ge(u_ok, 2 * a)
                else:
                    pe.wait_ge(att_ok, a)
                for j in range(2):
                    for k in range(KD):
                        mm = product(halves(2 - w)[:, j, :],
                                     both(wqkv, slice(None), k, slice(w * D + j * P, w * D + (j + 1) * P)),
                                     both(xaT, slice(None), k), k == 0, k == KD - 1)
                mm.then_inc(qk_ps, 1)

            def project_v(a):
                pe.wait_ge(trig, 2 * a + 1)
                for q in range(QT):
                    for k in range(KD):
                        mm = product(halves(2)[:, q, :], both(xaT, slice(None), k, slice(q * P, (q + 1) * P)),
                                     both(wqkv, slice(None), k, slice(2 * D, 3 * D)), k == 0, k == KD - 1)
                mm.then_inc(v_ps, 1)

            def scores(a, h):
                bk = h % 3
                if h == 0:
                    pe.wait_ge(stack_ld, 16 * 24 * (a + 1))
                    if not (isinstance(a, int) and a == 0):
                        pe.wait_ge(xbT_lo, 2 * a - 1)
                elif h == 1:
                    pe.wait_ge(trig, 2 * a + 2)
                elif h == 2:
                    pe.wait_ge(v_ok, a + 1)
                else:
                    pe.wait_ge(s_max, H * a + h - 2)
                pe.matmul(bank[:, bk, P:3 * P], ident_bf[:], causal_qk[:].rearrange("p a n -> p (a n)"),
                          start=True, stop=False, skip_group_check=True)
                rows = slice(64 * (h % 2), 64 * (h % 2) + STK)
                for q in (1, 0):
                    mm = pe.matmul(halves(bk)[:, 1 - q, :], q_stack[rows, h // 2, q * P:(q + 1) * P],
                                   k_stack[rows, h // 2, :], start=False, stop=(q == 0), skip_group_check=True)
                mm.then_inc(s_ps, 1)

            def transpose_max(a):
                pe.wait_ge(m_split, 2 * a + 2)
                for q in range(QT):
                    mm = pe.transpose(bank[0:32, 0, q * P:(q + 1) * P],
                                      mneg_s[:, q].rearrange("p a c h -> p (a c h)").bitcast(F32), ident[:])
                mm.then_inc(mT_ps, 1)

            def shifted(a, n):
                g, p = n // 2, n % 2
                if n == 0:
                    pe.wait_ge(shift_ld, 16 * 2 * (a + 1))
                if n >= 2:
                    pe.wait_ge(p_ok, H * a + n - 1)
                bk = n % 2
                pe.matmul(bank[:, bk, P:3 * P], ident_bf[:], causal_kq[:].rearrange("p a n -> p (a n)"),
                          start=True, stop=False, skip_group_check=True)
                rows = slice(64 * p, 64 * p + SX)
                for k in (1, 0):
                    mm = pe.matmul(halves(bk)[:, 1 - k, :], k_stack[rows, g, k * P:(k + 1) * P],
                                   q_stack[rows, g, :], start=False, stop=(k == 0), skip_group_check=True)
                mm.then_inc(st_ps, 1)

            def weigh(a, g):
                pe.wait_ge(p_ok, H * a + 4 * g + 4)
                if g == 0:
                    pe.wait_ge(v_ok, a + 1)
                if g == 2:
                    pe.wait_ge(u_ok, 2 * a + 1)
                dst = halves(2)[:, g % 2, :]
                for j in range(4):
                    pe.matmul(dst[32 * j:32 * j + 32, :], v_aug[:, 0, 4 * g + j, :],
                              probs[:, (4 * g + j) % 8, P:3 * P], start=True, stop=False, skip_group_check=True)
                for j in range(4):
                    mm = pe.matmul(dst[32 * j:32 * j + 32, P:T], v_aug[:, 1, 4 * g + j, :],
                                   probs[:, (4 * g + j) % 8, 0:P], start=False, stop=True, skip_group_check=True)
                mm.then_inc(pv_ps, 1)

            def turn_a(a):
                pe.wait_ge(u_ok, 2 * a + 2)
                for q in range(QT):
                    for g in range(4):
                        mm = pe.transpose(bank[:, q, g * P:(g + 1) * P], unnorm[:, g, q * P:(q + 1) * P], ident[:])
                mm.then_inc(ut_ps, 1)

            def turn_back_a(a):
                pe.wait_ge(att_ok, a + 1)
                for k in range(KD):
                    for q in range(QT):
                        mm = pe.transpose(bank[:, 0, k * T + q * P:k * T + (q + 1) * P],
                                          attn[:, q, k * P:(k + 1) * P], ident[:])
                mm.then_inc(atT_ps, 1)

            def output_a(a):
                pe.wait_ge(att_hi, a + 1)
                pe.wait_ge(att_lo, a + 1)
                for q in range(QT):
                    for k in range(KD):
                        mm = product(halves(0)[:, q, :], both(attn_s, slice(None), k, slice(q * P, (q + 1) * P)),
                                     both(wo, slice(None), k), k == 0, k == KD - 1)
                mm.then_inc(o_ps, 1)

            def transpose_b(b, n):
                pe.wait_ge(xn_b_ok, 2 * b + n + 1)
                for k in range(KD):
                    for q in range(QT):
                        mm = pe.transpose(bank[:, 7 * n, k * T + q * P:k * T + (q + 1) * P],
                                          xn_b[:, q, k * P:(k + 1) * P], ident[:])
                mm.then_inc(xbT_ps, 1)

            def queries(b, g):
                if g == 0:
                    pe.wait_ge(xbT_hi, 2 * b + 1)
                    pe.wait_ge(xbT_lo, 2 * b + 1)
                    pe.wait_ge(gl_ok, 4 * b)
                for c in range(2):
                    m = 2 * g + c
                    for k in range(KD):
                        mm = product(halves(3 + g)[:, c, :], both(wq2, slice(None), k, slice(m * P, (m + 1) * P)),
                                     both(xbT, slice(None), k), k == 0, k == KD - 1)
                mm.then_inc(q2_ps, 1)

            def scores2(b, g):
                if g == 0:
                    pe.wait_ge(q2_lo, 4 * b + 2)
                    pe.wait_ge(mask_ok, b + 1)
                    pe.wait_ge(k2_ld, 16 * 4 * (b + 1))
                else:
                    pe.wait_ge(q2_lo, 4 * b + 4)
                    pe.wait_ge(sub_ok, 4 * b + g)
                for c in range(2):
                    m = 2 * g + c
                    dst = halves(3 + c)
                    for q in range(QT):
                        pe.matmul(dst[:, q, 0:PAIR], ident_bf[:], mask_bf[:, q].rearrange("p a s -> p (a s)"),
                                  start=(q == 0), stop=False, skip_group_check=True)
                    for q in range(QT):
                        mm = product(dst[:, q, :], both(q2, slice(None), m, slice(q * P, (q + 1) * P)),
                                     both(k2, slice(None), slice(m * PAIR, m * PAIR + W)), False, q == QT - 1,
                                     skip_group_check=True)
                mm.then_inc(s2_ps, 1)

            def transpose2(b, g):
                pe.wait_ge(nrm_ok, 4 * b + g + 1)
                if g >= 1:
                    pe.wait_ge(c2_lo, 4 * b + g)
                for c in range(2):
                    for p in range(2):
                        for q in range(QT):
                            mm = pe.transpose(bank[0:S2, 5 + c, p * T + q * P:p * T + (q + 1) * P],
                                              sc2[g % 2][:, c * QT + q, p, :], ident[:])
                mm.then_inc(t2_ps, 1)

            def weigh2(b, g):
                pe.wait_ge(p2T_ok, 4 * b + g + 1)
                if g == 0:
                    pe.wait_ge(v2_ld, 16 * (b + 1))
                for c in range(2):
                    for j in range(4):
                        col = (2 * g + c) * P + 32 * j
                        mm = pe.matmul(halves(5)[32 * j:32 * j + 32, c, :], v2[:, col:col + 32],
                                       p2T[:, 2 * c + j // 2, :], start=True, stop=True, skip_group_check=True)
                mm.then_inc(c2_ps, 1)

            def output2(b, g):
                if g == 0:
                    pe.wait_ge(y_ok, b)
                pe.wait_ge(c2_hi, 4 * b + g + 1)
                pe.wait_ge(c2_lo, 4 * b + g + 1)
                for c in range(2):
                    m = 2 * g + c
                    for q in range(QT):
                        mm = product(halves(7)[:, q, :], both(c2, slice(None), c, slice(q * P, (q + 1) * P)),
                                     both(wo2, slice(None), m), m == 0 and q == 0, m == XM - 1,
                                     skip_group_check=True)
                mm.then_inc(o2_ps, 1)

            def hidden(b, g):
                if g == 0:
                    pe.wait_ge(xbT_hi, 2 * b + 2)
                    pe.wait_ge(xbT_lo, 2 * b + 2)
                    pe.wait_ge(c2_lo, 4 * b + 4)
                for c in range(2):
                    m = 2 * g + c
                    for k in range(KD):
                        mm = product(halves(3 + g)[:, c, :], both(wfc, slice(None), k, slice(m * P, (m + 1) * P)),
                                     both(xbT, slice(None), k), k == 0, k == KD - 1)
                mm.then_inc(fc_ps, 1)

            def project_down(b, g):
                pe.wait_ge(hid_lo, 4 * b + g + 1)
                for c in range(2):
                    m = 2 * g + c
                    for q in range(QT):
                        mm = product(halves(7)[:, q, :], both(hid, slice(None), m, slice(q * P, (q + 1) * P)),
                                     both(wpj, slice(None), m), m == 0 and q == 0, m == FM - 1,
                                     skip_group_check=True)
                if g == 3:
                    mm.then_inc(y_ps, 1)

            def first():
                pe.wait_ge(const_ok, 8)
                transpose_a(0)
                pe.wait_ge(w_lo, QKV_W + 1)
                project(0, 0)
                project(0, 1)
                project_v(0)

            def step(a, b, n):
                A, B, N = a is not None, b is not None, n is not None
                if B:
                    for g in range(3):
                        queries(b, g)
                    scores2(b, 0)
                    queries(b, 3)
                if A and not B:
                    for m in range(XM):
                        keys(m)
                if A:
                    for h in range(3):
                        scores(a, h)
                if B:
                    scores2(b, 1)
                if A:
                    scores(a, 3)
                if B:
                    transpose2(b, 0)
                if A:
                    scores(a, 4)
                    scores(a, 5)
                if B:
                    weigh2(b, 0)
                    scores2(b, 2)
                if A:
                    for h in range(6, 9):
                        scores(a, h)
                if B:
                    transpose2(b, 1)
                    output2(b, 0)
                if A:
                    scores(a, 9)
                    scores(a, 10)
                if B:
                    weigh2(b, 1)
                    scores2(b, 3)
                if A:
                    for h in range(11, 14):
                        scores(a, h)
                if B:
                    transpose2(b, 2)
                    output2(b, 1)
                if A:
                    scores(a, 14)
                    scores(a, 15)
                if B:
                    weigh2(b, 2)
                if A:
                    transpose_max(a)
                if B:
                    transpose2(b, 3)
                    output2(b, 2)
                if A and not B:
                    for t in range(VT):
                        values2(t)
                if B:
                    weigh2(b, 3)
                if N:
                    transpose_a(n)
                if B:
                    output2(b, 3)
                if A:
                    for h in range(6):
                        shifted(a, h)
                    if N:
                        pe.wait_ge(xaT_lo, n + 1)
                    weigh(a, 0)
                    shifted(a, 6)
                    shifted(a, 7)
                if B:
                    transpose_b(b, 1)
                if A:
                    for h in range(8, 12):
                        shifted(a, h)
                    weigh(a, 1)
                    shifted(a, 12)
                    shifted(a, 13)
                if B:
                    hidden(b, 0)
                if A:
                    shifted(a, 14)
                    shifted(a, 15)
                    weigh(a, 2)
                    weigh(a, 3)
                if B:
                    hidden(b, 1)
                if A:
                    turn_a(a)
                if N:
                    project(n, 0)
                if A:
                    turn_back_a(a)
                if N:
                    project(n, 1)
                if B:
                    hidden(b, 2)
                    hidden(b, 3)
                if A and not B:
                    lora_up()
                    lora_down()
                if A:
                    output_a(a)
                if N:
                    project_v(n)
                if B:
                    project_down(b, 0)
                    project_down(b, 1)
                if A:
                    if not B:
                        pe.wait_ge(w_lo, PJ_W + 1)
                    transpose_b(a, 0)
                if B:
                    project_down(b, 2)
                    project_down(b, 3)

            elements(first, step)(pe)

        @block.scalar
        def _(act):
            def split_hi(k):
                act.wait_ge(raw_sem[k], raw_count[k])
                if k == WV_W:
                    act.wait_ge(kx_ps, 2 * XM)
                if k == FC_W:
                    act.wait_ge(wstep, 6)
                if k == PJ_W:
                    act.wait_ge(wstep, 12)
                act.activation(split_to[k][0], raw_of[k], ACT.Copy).then_inc(w_hi, 1)

            def keys(m):
                if m == 0:
                    split_hi(WK_W)
                    split_hi(CTX_W)
                for n in (2 * m, 2 * m + 1):
                    act.wait_ge(kx_ps, n + 1)
                    if n >= 2:
                        act.wait_ge(kx_st[n % 2], 32 * (n // 2))
                    act.activation(k_out[n % 2][0], bank[:, 3 + n % 4, 0:HS], ACT.Copy).then_inc(kx_hi, 1)

            def values2():
                split_hi(WV_W)
                for n in range(2 * VT):
                    act.wait_ge(vx_ps, n + 1)
                    if n >= 2:
                        act.wait_ge(vx_st[n % 2], 16 * (n // 2))
                    rows = min(P, NS - n // 2 * P)
                    act.activation(v2w[0:rows, (n % 2) * 512:(n % 2 + 1) * 512], bank[0:rows, 3 + n % 4, :],
                                   ACT.Copy).then_inc(vx_ok, 1)
                split_hi(WQ_W)
                split_hi(WO2_W)

            def copy(dst, src, done):
                act.activation(dst, src, ACT.Copy).then_inc(done, 1)

            def xaT_part(a):
                act.wait_ge(xaT_ps, a + 1)
                act.wait_ge(v_ps, a)
                copy(xaT[0][:].rearrange("p k t -> p (k t)"), bank[:, 2, :], xaT_hi)

            def values(a):
                act.wait_ge(v_ps, a + 1)
                act.wait_ge(pv_ps, 4 * a)
                copy(v_aug[:, :, :, 0:DH], halves(2).rearrange("p q (h d) -> p q h d", h=H), v_ok)

            def rotated(a, w):
                act.wait_ge(rot_ok, 2 * a + w + 1)
                copy(rot_s[0][:, w], rot[:, w], rot_hi)

            def maxima(a):
                act.wait_ge(mT_ps, a + 1)
                act.wait_ge(shift_ld, 32 * a)
                copy(mnegT[:], bank[0:32, 0, 0:T], mT_ok)

            def exponentials(a, n):
                act.wait_ge(st_ps, H * a + n + 1)
                if n < 8:
                    if n == 0:
                        act.wait_ge(pv_ps, 4 * a)
                        act.wait_ge(rot_ok, 2 * a + 2)
                else:
                    act.wait_ge(pv_ps, 4 * a + n // 4 - 1)
                act.activation(probs[:, n % 8, :], bank[:, n % 2, P:4 * P], ACT.Exp, scale=SCALE).then_inc(p_ok, 1)

            def unnormalised(a, c):
                act.wait_ge(pv_ps, 4 * a + 2 * c + 2)
                if c == 0:
                    act.wait_ge(rot_lo, 2 * a + 2)
                copy(unnorm[:, 2 * c:2 * c + 2], halves(2), u_ok)

            def attention_hi(a):
                act.wait_ge(atT_ps, a + 1)
                copy(attn_s[0].rearrange("p k t -> p (k t)"), bank[:, 0, :], att_hi)

            def xbT_part(b, n):
                act.wait_ge(xbT_ps, 2 * b + n + 1)
                act.wait_ge(fc_ps if n == 0 else q2_ps, 4 * b + 4 * n)
                copy(xbT[0][:].rearrange("p k t -> p (k t)"), bank[:, 7 * n, :], xbT_hi)

            def queries(b, g):
                act.wait_ge(q2_ps, 4 * b + g + 1)
                if g == 0:
                    act.wait_ge(y_ps, b)
                copy(q2[0][:, 2 * g:2 * g + 2], halves(3 + g), q2_hi)

            def exponentials2(b, g):
                act.wait_ge(sub_ok, 4 * b + g + 1)
                act.activation(sc2[g % 2], sc2[g % 2], ACT.Exp, scale=XSCALE).then_inc(e2_ok, 1)

            def probabilities2(b, g):
                act.wait_ge(t2_ps, 4 * b + g + 1)
                if g == 0:
                    act.wait_ge(hid_lo, 4 * b)
                else:
                    act.wait_ge(c2_ps, 4 * b + g)
                copy(p2T.rearrange("p (c a) t -> p c (a t)", c=2), bank[0:S2, 5:7, :], p2T_ok)

            def context_hi(b, g):
                act.wait_ge(c2_ps, 4 * b + g + 1)
                act.wait_ge(o2_ps, 4 * b + g)
                copy(c2[0][:], halves(5), c2_hi)

            def hidden(b, g):
                act.wait_ge(fc_ps, 4 * b + g + 1)
                if g == 0:
                    act.wait_ge(c2_ps, 4 * b + 4)
                    act.wait_ge(s2_ps, 4 * b + 4)
                if g >= 2:
                    act.wait_ge(hid_lo, 4 * b + g - 1)
                for c in range(2):
                    m = 2 * g + c
                    last = act.activation(gl[:, g % 2, c, :], halves(3 + g)[:, c, :], ACT.Gelu,
                                          bias=bfc_t[:, m:m + 1])
                last.then_inc(gl_ok, 1)
                act.wait_ge(gl_ok, 4 * b + g + 1)
                copy(hid[0][:, 2 * g:2 * g + 2], gl[:, g % 2], hid_hi)

            def first():
                xaT_part(0)
                split_hi(QKV_W)
                rotated(0, 0)
                rotated(0, 1)
                values(0)
                act.wait_ge(const_ld, 16 * 4)
                split_hi(WO_W)

            def step(a, b, n):
                A, B, N = a is not None, b is not None, n is not None
                if B:
                    for g in range(4):
                        queries(b, g)
                    exponentials2(b, 0)
                    exponentials2(b, 1)
                    probabilities2(b, 0)
                    context_hi(b, 0)
                    exponentials2(b, 2)
                    probabilities2(b, 1)
                    context_hi(b, 1)
                    exponentials2(b, 3)
                    probabilities2(b, 2)
                    context_hi(b, 2)
                if A and not B:
                    for m in range(XM):
                        keys(m)
                if A:
                    maxima(a)
                if B:
                    probabilities2(b, 3)
                    context_hi(b, 3)
                if A and not B:
                    values2()
                if N:
                    xaT_part(n)
                if A:
                    for h in range(8):
                        exponentials(a, h)
                if B:
                    xbT_part(b, 1)
                if A:
                    for h in range(8, 12):
                        exponentials(a, h)
                    unnormalised(a, 0)
                    for h in range(12, 16):
                        exponentials(a, h)
                    unnormalised(a, 1)
                if B:
                    hidden(b, 0)
                if A:
                    attention_hi(a)
                if N:
                    rotated(n, 0)
                if B:
                    hidden(b, 1)
                if N:
                    rotated(n, 1)
                if A and not B:
                    split_hi(FC_W)
                    split_hi(PJ_W)
                if B:
                    hidden(b, 2)
                    hidden(b, 3)
                if N:
                    values(n)
                if A:
                    xbT_part(a, 0)

            elements(first, step)(act)

        @block.vector
        def _(dve):
            def split_lo(k):
                dve.wait_ge(w_hi, k + 1)
                dve.tensor_tensor(split_to[k][1], raw_of[k], split_to[k][0].bitcast(F32),
                                  ALU.subtract).then_inc(w_lo, 1)

            def quantise(n, k):
                w = raw_of[k]
                dve.wait_ge(raw_sem[k], raw_count[k])
                dve.tensor_reduce(wmax[:, 0:1], w, AX_X, ALU.max, apply_absolute_value=True).then_inc(wmax_ok, 1)
                dve.wait_ge(wmax_all, n + 1)
                dve.tensor_scalar(wscale[:, n:n + 1], wmax[:, 1:2], 1.0 / QMAX, None, ALU.mult).then_inc(wstep, 1)
                dve.wait_ge(wstep, 6 * n + 1)
                dve.reciprocal(winv[:, n:n + 1], wscale[:, n:n + 1]).then_inc(wstep, 1)
                dve.wait_ge(wstep, 6 * n + 2)
                dve.tensor_scalar(w, w, winv[:, n:n + 1], ROUND, ALU.mult, ALU.add).then_inc(wstep, 1)
                dve.wait_ge(wstep, 6 * n + 3)
                dve.tensor_scalar(w, w, ROUND, QMAX, ALU.subtract, ALU.min).then_inc(wstep, 1)
                dve.wait_ge(wstep, 6 * n + 4)
                dve.tensor_scalar(w, w, -QMAX - 1.0, wscale[:, n:n + 1], ALU.max, ALU.mult).then_inc(wstep, 1)
                dve.wait_ge(wstep, 6 * n + 5)
                dve.wait_ge(lora_ps, n + 1)
                dve.scalar_tensor_tensor(out=w, in0=bank[:, 3:7, :].rearrange("p b n -> p (b n)"), scalar=LORA_SCALE,
                                         in1=w, op0=ALU.mult, op1=ALU.add).then_inc(wstep, 1)

            def keys(m):
                if m == 0:
                    split_lo(WK_W)
                    split_lo(CTX_W)
                for n in (2 * m, 2 * m + 1):
                    dve.wait_ge(kx_hi, n + 1)
                    dve.tensor_tensor(k_out[n % 2][1], bank[:, 3 + n % 4, 0:HS], k_out[n % 2][0].bitcast(F32),
                                      ALU.subtract).then_inc(kx_lo, 1)

            def statistics(src, st, mv, rs, sems, ve_ok, n):
                st_ok, mv_ok, rs_ok, xn_ok = sems
                for q in range(QT):
                    last = dve.bn_stats(st[:, q, :], src[:, q, :])
                last.then_inc(st_ok, 1)
                dve.wait_ge(st_ok, n + 1)
                dve.sem_inc(waited_dve, 1)
                for q in range(QT):
                    last = dve.bn_aggr(mv[:, q, :], st[:, q, :])
                last.then_inc(mv_ok, 1)
                dve.wait_ge(mv_ok, n + 1)
                dve.tensor_scalar(rs[:], mv[:, :, 1:2], EPS, None, ALU.add).then_inc(ve_ok, 1)

            def norm(src, xn, mv, rs, sems, n):
                st_ok, mv_ok, rs_ok, xn_ok = sems
                dve.wait_ge(rs_ok, n + 1)
                for q in range(QT):
                    last = dve.tensor_scalar(xn[:, q, :], src[:, q, :], mv[:, q, 0:1], rs[:, q, :],
                                             ALU.subtract, ALU.mult)
                last.then_inc(xn_ok, 1)

            def low(dst, src, hi, done):
                dve.tensor_tensor(dst, src, hi.bitcast(F32), ALU.subtract).then_inc(done, 1)

            sems_a = (lna_st, lna_mv, lna_rs, xn_a_ok)
            sems_b = (lnb_st, lnb_mv, lnb_rs, xn_b_ok)

            def statistics_a(a):
                dve.wait_ge(x_ld, 16 * (a + 1))
                statistics(x_in, st_a, mv_a, rs_a, sems_a, lna_ve, a)

            def norm_a(a):
                dve.wait_ge(xaT_ps, a)
                norm(x_in, xn_a, mv_a, rs_a, sems_a, a)

            def xaT_part(a):
                dve.wait_ge(xaT_hi, a + 1)
                low(xaT[1][:].rearrange("p k t -> p (k t)"), bank[:, 2, :],
                    xaT[0][:].rearrange("p k t -> p (k t)"), xaT_lo)

            def rotary(a, w):
                dve.wait_ge(qk_ps, 2 * a + w + 1)
                if w == 0:
                    dve.wait_ge(pv_ps, 4 * a)
                    dve.wait_ge(const_ld, 16 * 4)
                else:
                    dve.wait_ge(rot_ok, 2 * a + w)
                for dst, table in ((tcos, cos_t), (tsin, sin_t)):
                    last = dve.tensor_tensor(dst, halves(2 - w),
                                             table[:].rearrange("p t -> p () t").broadcast_to([P, 2, T]), ALU.mult)
                last.then_inc(trig, 1)

            def maxima(a, h):
                dve.wait_ge(s_ps, H * a + h + 1)
                if h == 0:
                    dve.wait_ge(m_split, 2 * a)
                for q in range(QT):
                    off = (1 - q) * W
                    last = dve.tensor_reduce(mneg[:, q, h % 2, h // 2:h // 2 + 1], bank[:, h % 3, off:off + (q + 1) * P],
                                             AX_X, ALU.max, negate=True)
                last.then_inc(s_max, 1)

            def split_max(a):
                dve.wait_ge(s_max, H * a + H)
                dve.wait_ge(mT_ps, a)
                dve.tensor_copy(mneg_s[:, :, :, 0, :], mneg[:]).then_inc(m_split, 1)
                dve.wait_ge(m_split, 2 * a + 1)
                low(mneg_s[:, :, :, 1, :], mneg[:], mneg_s[:, :, :, 0, :], m_split)

            def attention(a):
                dve.wait_ge(ut_ps, a + 1)
                u = bank[:, 0:QT, :].rearrange("p q (h e) -> p q h e", h=H)
                dve.reciprocal(rc_a[:], u[:, :, :, DH]).then_inc(rca_ok, 1)
                dve.wait_ge(rca_ok, a + 1)
                for q in range(QT):
                    last = dve.tensor_tensor(attn[:, q, :].rearrange("p (h d) -> p h d", h=H), u[:, q, :, 0:DH],
                                             rc_a[:, q].rearrange("p h -> p h ()").broadcast_to([P, H, DH]), ALU.mult)
                last.then_inc(att_ok, 1)

            def attention_lo(a):
                dve.wait_ge(att_hi, a + 1)
                low(attn_s[1].rearrange("p k t -> p (k t)"), bank[:, 0, :],
                    attn_s[0].rearrange("p k t -> p (k t)"), att_lo)

            def residual_a(a):
                dve.wait_ge(o_ps, a + 1)
                dve.wait_ge(xres_ld, 16 * (a + 1))
                dve.wait_ge(x2_ok, a)
                dve.tensor_tensor(x1[:], halves(0), x_res[:], ALU.add).then_inc(x1_ok, 1)

            def mask_bias(b):
                dve.wait_ge(mask_ld, 16 * (b + 1))
                dve.wait_ge(s2_ps, 4 * b)
                for q in range(QT):
                    last = dve.tensor_scalar(mask_bf[:, q], mask_u8[:, q:q + 1, :].broadcast_to([P, 2, S2]),
                                             NEG, None, ALU.mult)
                last.then_inc(mask_ok, 1)

            def statistics_b(b, n):
                dve.wait_ge(x1_ok if n == 0 else x2_ok, b + 1)
                statistics(x1 if n == 0 else x2, st_b, mv_b, rs_b, sems_b, lnb_ve, 2 * b + n)

            def norm_b(b, n):
                dve.wait_ge(xbT_ps, 2 * b + n)
                norm(x1 if n == 0 else x2, xn_b, mv_b, rs_b, sems_b, 2 * b + n)

            def xbT_part(b, n):
                dve.wait_ge(xbT_hi, 2 * b + n + 1)
                low(xbT[1][:].rearrange("p k t -> p (k t)"), bank[:, 7 * n, :],
                    xbT[0][:].rearrange("p k t -> p (k t)"), xbT_lo)

            def queries(b, g):
                dve.wait_ge(q2_hi, 4 * b + g + 1)
                low(q2[1][:, 2 * g:2 * g + 2], halves(3 + g), q2[0][:, 2 * g:2 * g + 2], q2_lo)

            def softmax2(b, g):
                r = g % 2
                dve.wait_ge(s2_ps, 4 * b + g + 1)
                ps = bank[:, 3:5, :].rearrange("p c (q n) -> p (c q) n", q=2)[:, :, 0:PAIR] \
                    .rearrange("p g (a s) -> p g a s", a=2)
                dve.tensor_reduce(mx2[:, r], ps, AX_X, ALU.max).then_inc(mx2_ok, 1)
                dve.wait_ge(mx2_ok, 4 * b + g + 1)
                if g < 2:
                    dve.wait_ge(t2_ps, 4 * b)
                else:
                    dve.wait_ge(t2_ps, 4 * b + g - 1)
                dve.tensor_tensor(sc2[r], ps, mx2[:, r].rearrange("p g a -> p g a ()").broadcast_to([P, 4, 2, S2]),
                                  ALU.subtract).then_inc(sub_ok, 1)

            def sums2(b, g):
                r = g % 2
                dve.wait_ge(e2_ok, 4 * b + g + 1)
                dve.tensor_reduce(sm2[:, r], sc2[r], AX_X, ALU.add).then_inc(sm2_ok, 1)
                dve.wait_ge(sm2_ok, 4 * b + g + 1)
                dve.reciprocal(rc2[:, r], sm2[:, r]).then_inc(rc2_ok, 1)

            def context_lo(b, g):
                dve.wait_ge(c2_hi, 4 * b + g + 1)
                low(c2[1][:], halves(5), c2[0][:], c2_lo)

            def residual_b(b):
                dve.wait_ge(o2_ps, 4 * b + 4)
                dve.wait_ge(x2b_ok, b)
                dve.tensor_tensor(x2[:], halves(7), x1[:], ALU.add).then_inc(x2_ok, 1)

            def hidden_lo(b, g):
                dve.wait_ge(hid_hi, 4 * b + g + 1)
                low(hid[1][:, 2 * g:2 * g + 2], gl[:, g % 2], hid[0][:, 2 * g:2 * g + 2], hid_lo)

            def result(b):
                dve.wait_ge(y_ps, b + 1)
                dve.wait_ge(x2b_ok, b + 1)
                dve.wait_ge(y_st, 16 * b)
                dve.tensor_tensor(y, halves(7), x2b, ALU.add).then_inc(y_ok, 1)

            def first():
                statistics_a(0)
                norm_a(0)
                xaT_part(0)
                split_lo(QKV_W)
                rotary(0, 0)
                rotary(0, 1)
                split_lo(WO_W)

            def step(a, b, n):
                A, B, N = a is not None, b is not None, n is not None
                if B:
                    mask_bias(b)
                    for g in range(3):
                        queries(b, g)
                    softmax2(b, 0)
                    queries(b, 3)
                if A and not B:
                    for m in range(XM):
                        keys(m)
                if A:
                    maxima(a, 0)
                    maxima(a, 1)
                if B:
                    sums2(b, 0)
                    softmax2(b, 1)
                if A:
                    maxima(a, 2)
                    maxima(a, 3)
                if B:
                    sums2(b, 1)
                if A:
                    maxima(a, 4)
                    maxima(a, 5)
                if B:
                    context_lo(b, 0)
                if N:
                    statistics_a(n)
                if B:
                    softmax2(b, 2)
                if A:
                    for h in range(6, 9):
                        maxima(a, h)
                if B:
                    sums2(b, 2)
                if A:
                    maxima(a, 9)
                    maxima(a, 10)
                if B:
                    context_lo(b, 1)
                    softmax2(b, 3)
                if A:
                    for h in range(11, 14):
                        maxima(a, h)
                if B:
                    sums2(b, 3)
                if A:
                    maxima(a, 14)
                    maxima(a, 15)
                    split_max(a)
                if B:
                    context_lo(b, 2)
                if A and not B:
                    split_lo(WV_W)
                    split_lo(WQ_W)
                    split_lo(WO2_W)
                if N:
                    norm_a(n)
                if B:
                    context_lo(b, 3)
                if B:
                    residual_b(b)
                    statistics_b(b, 1)
                    norm_b(b, 1)
                if N:
                    xaT_part(n)
                if B:
                    xbT_part(b, 1)
                if A:
                    attention(a)
                if N:
                    rotary(n, 0)
                if A:
                    attention_lo(a)
                if N:
                    rotary(n, 1)
                if A and not B:
                    quantise(0, FC_W)
                    split_lo(FC_W)
                    quantise(1, PJ_W)
                    split_lo(PJ_W)
                if B:
                    hidden_lo(b, 0)
                    hidden_lo(b, 1)
                if A:
                    residual_a(a)
                    statistics_b(a, 0)
                if A:
                    norm_b(a, 0)
                if B:
                    hidden_lo(b, 2)
                    hidden_lo(b, 3)
                if A:
                    xbT_part(a, 0)
                if B:
                    result(b)

            elements(first, step)(dve)


IN_ORDER = ["x", "ctxT", "mask", "wqT", "wkT", "wvT", "woT", "wQ", "wK", "wV", "wO", "wfcT", "bfc", "Afc", "BfcT",
            "wpjT", "bpj", "Apj", "BpjT", "cos", "sin"]


def rotary_tables(tokens, head_width, repeat):
    half = head_width // 2
    theta = np.float32(10000.0) ** (np.float32(-2.0) * np.arange(half, dtype=np.float32) / np.float32(head_width))
    angles = np.arange(tokens, dtype=np.float32)[None, :] * theta.astype(np.float32)[:, None]
    rows = [np.tile(np.repeat(f(angles).astype(np.float32), repeat, axis=0), (2, 1)) for f in (np.cos, np.sin)]
    return rows


def kernel(x, ctx_1024, mask_BxSxS2_bk1, L0_attn_W_q, L0_attn_W_k, L0_attn_W_v, L0_attn_W_o, L0_xattn_W_Q,
           L0_xattn_W_K, L0_xattn_W_V, L0_xattn_W_O, L0_ffn_W_fc, L0_ffn_b_fc, L0_ffn_A_fc, L0_ffn_B_fc,
           L0_ffn_W_proj, L0_ffn_b_proj, L0_ffn_A_proj, L0_ffn_B_proj):
    import concourse.bacc as bacc
    from concourse.bass_utils import run_bass_kernel_spmd

    H = 16
    nb, tokens, d = x.shape
    hw = d // H

    def rotary_order(w):
        w = np.asarray(w).reshape(H // 2, 2, hw // 2, 2, d)
        return w.transpose(4, 3, 1, 2, 0).reshape(d, d)

    cos, sin = rotary_tables(tokens, hw, H // 2)
    f = L0_ffn_W_fc.shape[0]
    laid = {
        "x": x, "ctxT": np.asarray(ctx_1024).transpose(2, 0, 1).reshape(d, -1),
        "mask": np.asarray(mask_BxSxS2_bk1),
        "wqT": rotary_order(L0_attn_W_q), "wkT": rotary_order(L0_attn_W_k),
        "wvT": np.asarray(L0_attn_W_v).T, "woT": np.asarray(L0_attn_W_o).T,
        "wQ": L0_xattn_W_Q, "wK": L0_xattn_W_K, "wV": L0_xattn_W_V, "wO": L0_xattn_W_O,
        "wfcT": np.asarray(L0_ffn_W_fc).T, "bfc": np.asarray(L0_ffn_b_fc).reshape(f // P, P).T,
        "Afc": L0_ffn_A_fc, "BfcT": np.asarray(L0_ffn_B_fc).T,
        "wpjT": np.asarray(L0_ffn_W_proj).T, "bpj": np.asarray(L0_ffn_b_proj).reshape(1, d),
        "Apj": L0_ffn_A_proj, "BpjT": np.asarray(L0_ffn_B_proj).T, "cos": cos, "sin": sin,
    }
    nc = bacc.Bacc("TRN2", target_bir_lowering=False, num_devices=1)
    arrays, args = {}, []
    for name in IN_ORDER:
        a = np.ascontiguousarray(laid[name])
        arrays[f"in_{name}"] = a
        args.append(nc.dram_tensor(f"in_{name}", a.shape, mybir.dt.from_np(a.dtype), kind="ExternalInput").ap())
    out = nc.dram_tensor("out_y", x.shape, F32, kind="ExternalOutput").ap()
    decoder_layer(nc, *args, out)
    r = run_bass_kernel_spmd(nc, [arrays], core_ids=[0])
    return r.results[0]["out_y"]
```

```python
from contextlib import ExitStack

import numpy as np

import concourse.bass as bass
from concourse import mybir

P = 128
F32 = mybir.dt.float32
F32R = mybir.dt.float32r
BF16 = mybir.dt.bfloat16
U8 = mybir.dt.uint8
ALU = mybir.AluOpType
ACT = mybir.ActivationFunctionType
AX_X = mybir.AxisListType.X
RMAX = bass.bass_isa.ReduceOp.max

EPS = 1e-5
QMAX = 127.0
ROUND = 12582912.0
NEG = -float(2.0 ** 100)
LORA_SCALE = 2.0


def decoder_layer(nc, x, ctxT, mask, wqT, wkT, wvT, woT, wQ, wK, wV, wO, wfcT, bfc, Afc, BfcT,
                  wpjT, bpj, Apj, BpjT, cos, sin, out):
    NB, T, D = x.shape
    QT = T // P
    KD = D // P
    H = 16
    DH = D // H
    HH = H // 2
    HI = DH // 2
    S2 = mask.shape[2]
    XD = wQ.shape[1]
    XM = XD // P
    DX = XD // H
    R = Afc.shape[0]
    F = wfcT.shape[1]
    FM = F // P
    PAIR = 2 * S2
    W = 256
    STK = 3 * DH
    SX = STK + 2
    SCALE = float(DH) ** -0.5
    XSCALE = float(DX) ** -0.5

    with ExitStack() as ctx:
        def sb(name, shape, dt=F32):
            return ctx.enter_context(nc.sbuf_tensor(name, shape, dt))

        def sem(name):
            return ctx.enter_context(nc.semaphore(name))

        bank = ctx.enter_context(nc.psum_tensor("banks", [P, 8, 512], F32))

        def halves(b, w=W):
            return bank[:, b, :].rearrange("p (a n) -> p a n", n=w)

        ident = sb("ident", [P, P])
        ident_bf = sb("ident_bf", [P, P], BF16)
        causal_qk = sb("causal_qk", [P, 2, P], BF16)
        causal_kq = sb("causal_kq", [P, 2, P], BF16)
        cos_t = sb("cos_t", [P, T])
        sin_t = sb("sin_t", [P, T])
        bfc_t = sb("bfc_t", [P, FM])
        bpj_t = sb("bpj_t", [P, D])

        def pair(name, shape):
            return sb(name + "_hi", shape, F32R), sb(name + "_lo", shape, F32R)

        wqkv = pair("wqkv", [P, KD, 3 * D])
        wo = pair("wo", [P, KD, D])
        wq2 = pair("wq2", [P, KD, XD])
        wo2 = pair("wo2", [P, XM, D])
        wfc = pair("wfc", [P, KD, F])
        wpj = pair("wpj", [P, FM, D])

        x_in = sb("x_in", [P, QT, D])
        x_res = sb("x_res", [P, QT, D])
        xn_a = sb("xn_a", [P, QT, D])
        st_a = sb("st_a", [P, QT, 6])
        mv_a = sb("mv_a", [P, QT, 2])
        rs_a = sb("rs_a", [P, QT, 1])
        half_a = sb("half_a", [P, QT, 1])
        xaT = pair("xaT", [P, KD, T])
        rot = sb("rot", [P, 2, 2, T])
        rot_s = pair("rot_s", [P, 2, 2, T])
        unnorm = rot[:].rearrange("p a b t -> p (a b) t")
        attn = sb("attn", [P, QT, D])
        attn_s = [v[:] for v in pair("attn", [P, KD, T])]
        rc_a = sb("rc_a", [P, QT, H])
        q_stack = sb("q_stack", [P, HH, T], F32R)
        k_stack = sb("k_stack", [P, HH, T], F32R)
        v_aug = sb("v_aug", [P, QT, H, 32])
        probs = sb("probs", [P, 8, 3 * P])
        tcos = probs[:, 0:4, :].rearrange("p a b -> p (a b)")[:, 0:2 * T].rearrange("p (j t) -> p j t", j=2)
        tsin = probs[:, 4:8, :].rearrange("p a b -> p (a b)")[:, 0:2 * T].rearrange("p (j t) -> p j t", j=2)
        mneg = sb("mneg", [P, QT, 2, HH])
        mneg_s = sb("mneg_s", [P, QT, 2, 2, HH], F32R)
        mnegT = sb("mnegT", [32, T], F32R)
        x1 = sb("x1", [P, QT, D])

        x2 = sb("x2", [P, QT, D])
        st_b = sb("st_b", [P, QT, 6])
        mv_b = sb("mv_b", [P, QT, 2])
        rs_b = sb("rs_b", [P, QT, 1])
        xbT = pair("xbT", [P, KD, T])
        q2 = pair("q2", [P, XM, T])
        hid = q2
        KW = (XM - 1) * PAIR + W
        k2 = pair("k2", [P, KW])
        v2w = sb("v2", [P, XD])
        v2 = v2w[0:S2]
        mask_u8 = sb("mask_u8", [P, QT, S2], U8)
        mask_bf = sb("mask_bf", [P, QT, 2, S2], BF16)
        mx2 = sb("mx2", [P, 2, 4, 2])
        sm2 = sb("sm2", [P, 2, 4, 2])
        rc2 = sb("rc2", [P, 2, 4, 2])
        c2 = pair("c2", [P, 2, T])
        LOAD = KD * XD
        work = sb("work", [P, max(2 * LOAD, 4 * T + 16 * S2 + 3 * QT * D)])
        o = 4 * T
        p2T = work[0:S2, 0:o].rearrange("p (h t) -> p h t", t=T)
        gl = work[:, 0:o].rearrange("p (r a t) -> p r a t", r=2, t=T)
        sc2 = [work[:, o + r * 8 * S2:o + (r + 1) * 8 * S2].rearrange("p (g a s) -> p g a s", g=4, s=S2)
               for r in range(2)]
        o += 16 * S2
        x2b, xn_b, y = (work[:, o + j * QT * D:o + (j + 1) * QT * D].rearrange("p (q d) -> p q d", q=QT)
                        for j in range(3))

        NS = NB * S2
        HS = NS // 2
        VT = -(-NS // P)
        raw = [work[:, 0:LOAD], work[:, LOAD:2 * LOAD]]
        wk2 = [v[:].rearrange("p m t -> p (m t)").rearrange("p (k n) -> p k n", k=KD) for v in q2]
        ctx_s = [v[:, 0:KD * NS].rearrange("p (k n) -> p k n", k=KD) for v in k2]
        KG = KD * F // NS
        k_stage = [[v[:].rearrange("p k n -> p (k n)")[:, 0:KG * NS].rearrange("p (m n) -> p m n", n=NS) for v in pr]
                   for pr in (wfc, wpj, wo2)]
        lora_b = probs[0:R].rearrange("p a b -> p (a b)")[:, 0:F]
        v_stage = [v2w[:], rot[:].rearrange("p a b t -> p (a b t)")] + [
            probs[:].rearrange("p a b -> p (a b)")[:, r * XD:(r + 1) * XD] for r in (1, 2)]
        VR = len(v_stage)
        wmax = sb("wmax", [P, 2])
        wscale = sb("wscale", [P, 2])
        winv = sb("winv", [P, 2])

        k2_dram = nc.dram_tensor("k2_dram", [2, P, XM, NS], F32, kind="Internal").ap()
        v2_dram = nc.dram_tensor("v2_dram", [NS, XD], F32, kind="Internal").ap()

        block = ctx.enter_context(nc.Block())

        const_ld, const_ok, k2_zero = sem("const_ld"), sem("const_ok"), sem("k2_zero")
        raw_ld = [sem(f"raw{r}_ld") for r in range(2)] + [sem(f"raw{r}_reld") for r in range(2)]
        w_hi, w_lo = sem("w_hi"), sem("w_lo")
        kx_ps, kx_hi, kx_lo, kx_st = sem("kx_ps"), sem("kx_hi"), sem("kx_lo"), sem("kx_st")
        vx_ps, vx_ok, vx_st = sem("vx_ps"), sem("vx_ok"), [sem(f"vx_st{r}") for r in range(VR)]
        lora_up_ld, lora_down_ld, lora_ps = sem("lora_up_ld"), sem("lora_down_ld"), sem("lora_ps")
        wmax_ok, wmax_all, wstep = sem("wmax_ok"), sem("wmax_all"), sem("wstep")
        waited_sp, waited_dve = sem("waited_sp"), sem("waited_dve")
        x_ld, xres_ld = sem("x_ld"), sem("xres_ld")
        lna_st, lna_mv, lna_rs, xn_a_ok = sem("lna_st"), sem("lna_mv"), sem("lna_rs"), sem("xn_a_ok")
        xaT_ps, xaT_hi, xaT_lo = sem("xaT_ps"), sem("xaT_hi"), sem("xaT_lo")
        qk_ps, v_ps, v_ok = sem("qk_ps"), sem("v_ps"), sem("v_ok")
        trig, rot_ok, rot_hi, rot_lo = sem("trig"), sem("rot_ok"), sem("rot_hi"), sem("rot_lo")
        stack_ld, shift_ld = sem("stack_ld"), sem("shift_ld")
        s_ps, s_max = sem("s_ps"), sem("s_max")
        m_split, mT_ps, mT_ok = sem("m_split"), sem("mT_ps"), sem("mT_ok")
        st_ps, p_ok, pv_ps = sem("st_ps"), sem("p_ok"), sem("pv_ps")
        u_ok, ut_ps, rca_ok, att_ok = sem("u_ok"), sem("ut_ps"), sem("rca_ok"), sem("att_ok")
        atT_ps, att_hi, att_lo = sem("atT_ps"), sem("att_hi"), sem("att_lo")
        lna_ve, lnb_ve = sem("lna_ve"), sem("lnb_ve")
        o_ps, x1_ok = sem("o_ps"), sem("x1_ok")
        lnb_st, lnb_mv, lnb_rs, xn_b_ok = sem("lnb_st"), sem("lnb_mv"), sem("lnb_rs"), sem("xn_b_ok")
        xbT_ps, xbT_hi, xbT_lo = sem("xbT_ps"), sem("xbT_hi"), sem("xbT_lo")
        mask_ld, mask_ok, k2_ld, v2_ld = sem("mask_ld"), sem("mask_ok"), sem("k2_ld"), sem("v2_ld")
        q2_ps, q2_hi, q2_lo = sem("q2_ps"), sem("q2_hi"), sem("q2_lo")
        s2_ps, mx2_ok, sub_ok, e2_ok = sem("s2_ps"), sem("mx2_ok"), sem("sub_ok"), sem("e2_ok")
        sm2_ok, rc2_ok, nrm_ok = sem("sm2_ok"), sem("rc2_ok"), sem("nrm_ok")
        t2_ps, p2T_ok, c2_ps, c2_hi, c2_lo = (sem(n) for n in ("t2_ps", "p2T_ok", "c2_ps", "c2_hi", "c2_lo"))
        o2_ps, x2_ok, x2b_ok = sem("o2_ps"), sem("x2_ok"), sem("x2b_ok")
        fc_ps, gl_ok, hid_hi, hid_lo = sem("fc_ps"), sem("gl_ok"), sem("hid_hi"), sem("hid_lo")
        y_ps, y_ok, y_st = sem("y_ps"), sem("y_ok"), sem("y_st")

        def shifted_bank(a, n):
            ring = (0, 1) if isinstance(a, int) and a == 0 else (0, 1, 5, 6)
            return len(ring), ring[n % len(ring)]

        def elements(first, step):
            def run(eng):
                first()
                step(0, None, 1, 2)
                step(1, 0, 2, 3)
                with eng.Fori(2, NB - 2) as i:
                    step(i, i - 1, i + 1, i + 2)
                step(NB - 2, NB - 3, NB - 1, None)
                step(NB - 1, NB - 2, None, None)
                step(None, NB - 1, None, None)
            return run

        N_CONST = 5
        QKV_W, WK_W, CTX_W, WV_W, WO_W, WO2_W, FC_W, WQ_W, PJ_W = range(9)
        K_GROUPS = [(g, min(KG, XM - g)) for g in range(0, XM, KG)]
        split_to = [[v[:].rearrange("p k n -> p (k n)") for v in wqkv],
                    [v.rearrange("p k n -> p (k n)") for v in wk2],
                    [v[:, 0:KD * NS] for v in k2]] + [
                    [v[:].rearrange("p k n -> p (k n)") for v in pr] for pr in (wq2, wo, wo2, wfc, wq2, wpj)]
        raw_of = [raw[k % 2][:, 0:split_to[k][0].shape[1]] for k in range(9)]
        V_STORES = [16 * len(range(r, VT, VR)) for r in range(VR)]
        RAW_DMAS = [3, 1, 1, 1, 1, 1, 1, 1, 1]
        raw_sem = [raw_ld[k] if k < 2 else raw_ld[2 + k % 2] for k in range(9)]
        raw_count = [16 * RAW_DMAS[k] if k < 2 else 16 * (k // 2) for k in range(9)]

        def load_raw(eng, k, *views):
            if k >= 2:
                eng.wait_ge(w_lo, k - 1)
            for dst, src in views:
                eng.dma_start(dst, src).then_inc(raw_sem[k], 16)

        def tiles(k, n):
            return raw_of[k].rearrange("p (k n) -> p k n", n=n)

        def rows(w):
            return w.rearrange("(k p) n -> p k n", p=P)

        @block.sync
        def _(sp):
            sp.dma_start(x_in[:], x[0].rearrange("(q p) d -> p q d", p=P)).then_inc(x_ld, 16)
            load_raw(sp, QKV_W, *[(tiles(QKV_W, 3 * D)[:, :, j * D:(j + 1) * D], rows(w))
                              for j, w in enumerate((wqT, wkT, wvT))])
            load_raw(sp, WK_W, (tiles(WK_W, XD), rows(wK)))
            sp.dma_start(cos_t[:], cos).then_inc(const_ld, 16)
            sp.dma_start(sin_t[:], sin).then_inc(const_ld, 16)
            sp.dma_start(bfc_t[:], bfc).then_inc(const_ld, 16)
            sp.dma_start(bpj_t[:], bpj.broadcast_to([P, D])).then_inc(const_ld, 16)

            def load_x(n):
                sp.wait_ge(xn_a_ok, n)
                sp.sem_inc(waited_sp, 1)
                sp.dma_start(x_in[:], x[n].rearrange("(q p) d -> p q d", p=P)).then_inc(x_ld, 16)

            def stacks(n):
                for w, (stack, order) in enumerate(((q_stack, (0, 0, 1)), (k_stack, (0, 1, 0)))):
                    if w == 0:
                        sp.wait_ge(st_ps, H * n)
                    for piece, done in ((0, rot_hi), (1, rot_lo)):
                        sp.wait_ge(done, 2 * n + w + 1)
                        for c in range(3):
                            if order[c] != piece:
                                continue
                            for p in range(2):
                                for j in range(2):
                                    row = 64 * p + c * DH + j * HI
                                    sp.dma_start(stack[row:row + HI, :, :].bitcast(F32),
                                                 rot_s[piece][64 * p:64 * p + 64, w, j, :].bitcast(F32)
                                                 ).then_inc(stack_ld, 16)

            def context(b):
                if isinstance(b, int) and b == 0:
                    sp.wait_ge(kx_st, 16 * 2 * len(K_GROUPS))
                    sp.wait_ge(k2_zero, 1)
                sp.wait_ge(mask_ok, b)
                sp.sem_inc(waited_sp, 1)
                sp.dma_start(mask_u8[:], mask[b].rearrange("(q p) s -> p q s", p=P)).then_inc(mask_ld, 16)
                sp.wait_ge(s2_ps, 4 * b)
                sp.sem_inc(waited_sp, 1)
                for piece in range(2):
                    for p in range(2):
                        dst = k2[piece][64 * p:64 * p + DX, 0:XM * PAIR].bitcast(F32)
                        sp.dma_start(
                            dst.rearrange("p (m a s) -> p m a s", a=2, s=S2)[:, :, p, :],
                            k2_dram[piece, 64 * p:64 * p + DX].rearrange("p m (b s) -> p m b s", s=S2)[:, :, b, :]
                        ).then_inc(k2_ld, 16)

            def context_values(b):
                if isinstance(b, int) and b == 0:
                    for r in range(VR):
                        sp.wait_ge(vx_st[r], V_STORES[r])
                    sp.wait_ge(lora_ps, 2)
                sp.wait_ge(c2_ps, 4 * b)
                sp.sem_inc(waited_sp, 1)
                sp.dma_start(v2, v2_dram.rearrange("(b s) n -> b s n", s=S2)[b]).then_inc(v2_ld, 16)

            def first():
                load_x(1)
                stacks(0)

            def step(a, b, n, m):
                if a is not None:
                    sp.wait_ge(x1_ok, a)
                    sp.sem_inc(waited_sp, 1)
                    sp.dma_start(x_res[:], x[a].rearrange("(q p) d -> p q d", p=P)).then_inc(xres_ld, 16)
                    if m is not None:
                        load_x(m)
                    sp.wait_ge(mT_ok, a + 1)
                    for p in range(2):
                        sp.dma_start(q_stack[64 * p + STK:64 * p + SX, :, :].bitcast(F32),
                                     mnegT[p * H:(p + 1) * H, :].bitcast(F32)).then_inc(shift_ld, 16)
                    context(a)
                if n is not None:
                    stacks(n)
                if a is not None:
                    context_values(a)

            elements(first, step)(sp)

        @block.gpsimd
        def _(pool):
            pool.memset(ident[:], 0.0)
            pool.memset(causal_qk[:], 0.0)
            pool.memset(causal_kq[:], 0.0).then_inc(const_ok, 1)
            pool.wait_ge(const_ok, 1)
            pool.affine_select(out=ident[:], in_=ident[:], compare_op=ALU.not_equal, fill=1.0, base=0,
                               pattern=[[-1, P]], channel_multiplier=1).then_inc(const_ok, 1)
            pool.affine_select(out=causal_qk[:], in_=causal_qk[:], compare_op=ALU.is_ge, fill=NEG, base=0,
                               pattern=[[0, 2], [-1, P]], channel_multiplier=1).then_inc(const_ok, 1)
            pool.affine_select(out=causal_kq[:], in_=causal_kq[:], compare_op=ALU.is_ge, fill=NEG, base=0,
                               pattern=[[0, 2], [1, P]], channel_multiplier=-1).then_inc(const_ok, 1)
            pool.wait_ge(const_ok, 2)
            pool.tensor_copy(ident_bf[:], ident[:]).then_inc(const_ok, 1)
            pool.memset(half_a[:], -0.5)
            pool.memset(v_aug[:], 0.0).then_inc(const_ok, 1)
            pool.wait_ge(const_ok, 6)
            pool.memset(v_aug[:, :, :, DH:DH + 1], 1.0).then_inc(const_ok, 1)
            pool.memset(k_stack[:].bitcast(F32), 1.0).then_inc(const_ok, 1)

            def quantiser(n):
                pool.wait_ge(wmax_ok, n + 1)
                pool.partition_all_reduce(wmax[:, 1:2], wmax[:, 0:1], P, RMAX).then_inc(wmax_all, 1)
                pool.wait_ge(wstep, 6 * n + 1)

            def start_b():
                def store_keys(c):
                    m, count = K_GROUPS[c]
                    pool.wait_ge(kx_lo, 2 * (m + count))
                    for piece in range(2):
                        pool.dma_start(k2_dram[piece, :, m:m + count, :],
                                       k_stage[c][piece][:, 0:count].bitcast(F32)).then_inc(kx_st, 16)

                def store_values(t):
                    rows_t = min(P, NS - t * P)
                    pool.wait_ge(vx_ok, 2 * t + 2)
                    pool.dma_start(v2_dram[t * P:t * P + rows_t, :], v_stage[t % VR][0:rows_t]).then_inc(vx_st[t % VR], 16)

                load_raw(pool, WO_W, (tiles(WO_W, D), rows(woT)))
                pool.dma_start(x2[0:R, 0, :], Afc).then_inc(lora_up_ld, 16)
                pool.dma_start(lora_b, BfcT).then_inc(lora_up_ld, 16)
                load_raw(pool, WO2_W, (tiles(WO2_W, D), rows(wO)))
                load_raw(pool, FC_W, (tiles(FC_W, F), rows(wfcT)))
                store_keys(0)
                store_values(0)
                quantiser(0)
                store_values(1)
                for c in range(1, len(K_GROUPS)):
                    store_keys(c)
                for t in range(2, VT):
                    store_values(t)
                for v in k2:
                    last = pool.memset(v[:].bitcast(F32), 0.0)
                last.then_inc(k2_zero, 1)
                pool.dma_start(x2[0:R, 1, :], BpjT).then_inc(lora_down_ld, 16)
                pool.wait_ge(vx_st[0], V_STORES[0])
                pool.dma_start(v2[0:R, :], Apj).then_inc(lora_down_ld, 16)
                load_raw(pool, WQ_W, (tiles(WQ_W, XD), rows(wQ)))
                load_raw(pool, PJ_W, (tiles(PJ_W, D), rows(wpjT)))

            def rotate(a, w):
                pool.wait_ge(trig, 2 * a + w + 1)
                if w == 0:
                    pool.wait_ge(ut_ps, a)
                pool.tensor_tensor(rot[:, w, 0, :], tcos[:, 0, :], tsin[:, 1, :], ALU.subtract)
                pool.tensor_tensor(rot[:, w, 1, :], tcos[:, 1, :], tsin[:, 0, :], ALU.add).then_inc(rot_ok, 1)
                pool.wait_ge(rot_hi, 2 * a + w + 1)
                pool.wait_ge(rot_ok, 2 * a + w + 1)
                pool.tensor_tensor(rot_s[1][:, w], rot[:, w], rot_s[0][:, w].bitcast(F32),
                                   ALU.subtract).then_inc(rot_lo, 1)

            def inverse_deviation(rs, ve_ok, rs_ok, n):
                pool.wait_ge(ve_ok, n + 1)
                pool.tensor_tensor(rs[:], rs[:], half_a[:], ALU.pow).then_inc(rs_ok, 1)

            def normalise(b, g):
                pool.wait_ge(rc2_ok, 4 * b + g + 1)
                pool.tensor_tensor(sc2[g % 2], sc2[g % 2],
                                   rc2[:, g % 2].rearrange("p g a -> p g a ()").broadcast_to([P, 4, 2, S2]),
                                   ALU.mult).then_inc(nrm_ok, 1)

            def residual_bias(b):
                pool.wait_ge(x2_ok, b + 1)
                pool.wait_ge(y_ok, b)
                for q in range(QT):
                    last = pool.tensor_tensor(x2b[:, q, :], x2[:, q, :], bpj_t[:], ALU.add)
                last.then_inc(x2b_ok, 1)

            def first():
                inverse_deviation(rs_a, lna_ve, lna_rs, 0)
                load_raw(pool, CTX_W, (tiles(CTX_W, NS), rows(ctxT)))
                load_raw(pool, WV_W, (tiles(WV_W, XD), rows(wV)))
                rotate(0, 0)
                rotate(0, 1)
                inverse_deviation(rs_a, lna_ve, lna_rs, 1)
                start_b()

            def step(a, b, n, m):
                A, B, N, M = (e is not None for e in (a, b, n, m))
                if B:
                    normalise(b, 0)
                    normalise(b, 1)
                if B:
                    normalise(b, 2)
                    normalise(b, 3)
                    inverse_deviation(rs_b, lnb_ve, lnb_rs, 2 * b + 1)
                    residual_bias(b)
                if M:
                    inverse_deviation(rs_a, lna_ve, lna_rs, m)
                if A and not B:
                    quantiser(1)
                if N:
                    rotate(n, 0)
                    rotate(n, 1)
                if A:
                    inverse_deviation(rs_b, lnb_ve, lnb_rs, 2 * a)
                if B:
                    pool.wait_ge(y_ok, b + 1)
                    pool.dma_start(out[b].rearrange("(q p) d -> p q d", p=P), y).then_inc(y_st, 16)

            elements(first, step)(pool)
            pool.wait_ge(y_st, 16 * NB)

        @block.tensor
        def _(pe):
            def product(dst, w, x_, first, last, **kw):
                pe.matmul(dst, w[0], x_[0], start=first, stop=False, **kw)
                pe.matmul(dst, w[0], x_[1], start=False, stop=False, **kw)
                return pe.matmul(dst, w[1], x_[0], start=False, stop=last, **kw)

            def both(pr, *index):
                return [v[index] for v in pr]

            def keys(m):
                if m == 0:
                    pe.wait_ge(w_lo, CTX_W + 1)
                for half in range(2):
                    n = 2 * m + half
                    if n >= 4:
                        pe.wait_ge(kx_lo, n - 3)
                    for k in range(KD):
                        mm = product(bank[:, 3 + n % 4, 0:HS], both(wk2, slice(None), k, slice(m * P, m * P + P)),
                                     both(ctx_s, slice(None), k, slice(half * HS, (half + 1) * HS)),
                                     k == 0, k == KD - 1)
                    mm.then_inc(kx_ps, 1)

            def values2(t):
                if t == 0:
                    pe.wait_ge(w_lo, WV_W + 1)
                    pe.wait_ge(kx_lo, 2 * XM)
                rows = min(P, NS - t * P)
                for half in range(2):
                    n = 2 * t + half
                    if n >= 4:
                        pe.wait_ge(vx_ok, n - 3)
                    for k in range(KD):
                        mm = product(bank[0:rows, 3 + n % 4, :], both(ctx_s, slice(None), k, slice(t * P, t * P + rows)),
                                     both(wq2, slice(None), k, slice(half * 512, (half + 1) * 512)),
                                     k == 0, k == KD - 1)
                    mm.then_inc(vx_ps, 1)

            def lora_up():
                pe.wait_ge(vx_ok, 2 * VT)
                pe.wait_ge(lora_up_ld, 16 * 2)
                for k in range(KD):
                    for half in range(2):
                        mm = pe.matmul(bank[:, 3 + 2 * k + half, :], x2[0:R, 0, k * P:(k + 1) * P],
                                       lora_b[:, half * 512:(half + 1) * 512], start=True, stop=True)
                mm.then_inc(lora_ps, 1)

            def lora_down():
                pe.wait_ge(lora_down_ld, 16 * 2)
                pe.wait_ge(wstep, 6)
                for m in range(FM):
                    mm = pe.matmul(bank[:, 3 + m // 2, (m % 2) * D:(m % 2 + 1) * D], v2[0:R, m * P:(m + 1) * P],
                                   x2[0:R, 1, :], start=True, stop=True)
                mm.then_inc(lora_ps, 1)

            def transpose_a(a):
                pe.wait_ge(xn_a_ok, a + 1)
                for k in range(KD):
                    for q in range(QT):
                        mm = pe.transpose(bank[:, 2, k * T + q * P:k * T + (q + 1) * P],
                                          xn_a[:, q, k * P:(k + 1) * P], ident[:])
                mm.then_inc(xaT_ps, 1)

            def project(a, w):
                if w == 0:
                    pe.wait_ge(xaT_hi, a + 1)
                    pe.wait_ge(xaT_lo, a + 1)
                    pe.wait_ge(u_ok, 2 * a)
                else:
                    pe.wait_ge(att_ok, a)
                for j in range(2):
                    for k in range(KD):
                        mm = product(halves(2 - w)[:, j, :],
                                     both(wqkv, slice(None), k, slice(w * D + j * P, w * D + (j + 1) * P)),
                                     both(xaT, slice(None), k), k == 0, k == KD - 1)
                mm.then_inc(qk_ps, 1)

            def project_v(a):
                pe.wait_ge(trig, 2 * a + 1)
                for q in range(QT):
                    for k in range(KD):
                        mm = product(halves(2)[:, q, :], both(xaT, slice(None), k, slice(q * P, (q + 1) * P)),
                                     both(wqkv, slice(None), k, slice(2 * D, 3 * D)), k == 0, k == KD - 1)
                mm.then_inc(v_ps, 1)

            def scores(a, h):
                bk = h % 3
                if h == 0:
                    pe.wait_ge(stack_ld, 16 * 24 * (a + 1))
                    if not (isinstance(a, int) and a == 0):
                        pe.wait_ge(xbT_lo, 2 * a - 1)
                elif h == 1:
                    pe.wait_ge(trig, 2 * a + 2)
                elif h == 2:
                    pe.wait_ge(v_ok, a + 1)
                else:
                    pe.wait_ge(s_max, H * a + h - 2)
                pe.matmul(bank[:, bk, P:3 * P], ident_bf[:], causal_qk[:].rearrange("p a n -> p (a n)"),
                          start=True, stop=False, skip_group_check=True)
                rows = slice(64 * (h % 2), 64 * (h % 2) + STK)
                for q in (1, 0):
                    mm = pe.matmul(halves(bk)[:, 1 - q, :], q_stack[rows, h // 2, q * P:(q + 1) * P],
                                   k_stack[rows, h // 2, :], start=False, stop=(q == 0), skip_group_check=True)
                mm.then_inc(s_ps, 1)

            def transpose_max(a):
                pe.wait_ge(m_split, 2 * a + 2)
                for q in range(QT):
                    mm = pe.transpose(bank[0:32, 0, q * P:(q + 1) * P],
                                      mneg_s[:, q].rearrange("p a c h -> p (a c h)").bitcast(F32), ident[:])
                mm.then_inc(mT_ps, 1)

            def shifted(a, n):
                g, p = n // 2, n % 2
                if n == 0:
                    pe.wait_ge(shift_ld, 16 * 2 * (a + 1))
                ring, bk = shifted_bank(a, n)
                if n >= ring:
                    pe.wait_ge(p_ok, H * a + n + 1 - ring)
                pe.matmul(bank[:, bk, P:3 * P], ident_bf[:], causal_kq[:].rearrange("p a n -> p (a n)"),
                          start=True, stop=False, skip_group_check=True)
                rows = slice(64 * p, 64 * p + SX)
                for k in (1, 0):
                    mm = pe.matmul(halves(bk)[:, 1 - k, :], k_stack[rows, g, k * P:(k + 1) * P],
                                   q_stack[rows, g, :], start=False, stop=(k == 0), skip_group_check=True)
                mm.then_inc(st_ps, 1)

            def weigh(a, g):
                pe.wait_ge(p_ok, H * a + 4 * g + 4)
                if g == 0:
                    pe.wait_ge(v_ok, a + 1)
                if g == 2:
                    pe.wait_ge(u_ok, 2 * a + 1)
                dst = halves(2)[:, g % 2, :]
                for j in range(4):
                    pe.matmul(dst[32 * j:32 * j + 32, :], v_aug[:, 0, 4 * g + j, :],
                              probs[:, (4 * g + j) % 8, P:3 * P], start=True, stop=False, skip_group_check=True)
                for j in range(4):
                    mm = pe.matmul(dst[32 * j:32 * j + 32, P:T], v_aug[:, 1, 4 * g + j, :],
                                   probs[:, (4 * g + j) % 8, 0:P], start=False, stop=True, skip_group_check=True)
                mm.then_inc(pv_ps, 1)

            def turn_a(a):
                pe.wait_ge(u_ok, 2 * a + 2)
                for q in range(QT):
                    for g in range(4):
                        mm = pe.transpose(bank[:, q, g * P:(g + 1) * P], unnorm[:, g, q * P:(q + 1) * P], ident[:])
                mm.then_inc(ut_ps, 1)

            def turn_back_a(a):
                pe.wait_ge(att_ok, a + 1)
                for k in range(KD):
                    for q in range(QT):
                        mm = pe.transpose(bank[:, 0, k * T + q * P:k * T + (q + 1) * P],
                                          attn[:, q, k * P:(k + 1) * P], ident[:])
                mm.then_inc(atT_ps, 1)

            def output_a(a):
                pe.wait_ge(att_hi, a + 1)
                pe.wait_ge(att_lo, a + 1)
                for q in range(QT):
                    for k in range(KD):
                        mm = product(halves(0)[:, q, :], both(attn_s, slice(None), k, slice(q * P, (q + 1) * P)),
                                     both(wo, slice(None), k), k == 0, k == KD - 1)
                mm.then_inc(o_ps, 1)

            def transpose_b(b, n):
                pe.wait_ge(xn_b_ok, 2 * b + n + 1)
                for k in range(KD):
                    for q in range(QT):
                        mm = pe.transpose(bank[:, 7 * n, k * T + q * P:k * T + (q + 1) * P],
                                          xn_b[:, q, k * P:(k + 1) * P], ident[:])
                mm.then_inc(xbT_ps, 1)

            def queries(b, g):
                if g == 0:
                    pe.wait_ge(xbT_hi, 2 * b + 1)
                    pe.wait_ge(xbT_lo, 2 * b + 1)
                    pe.wait_ge(gl_ok, 4 * b)
                for c in range(2):
                    m = 2 * g + c
                    for k in range(KD):
                        mm = product(halves(3 + g)[:, c, :], both(wq2, slice(None), k, slice(m * P, (m + 1) * P)),
                                     both(xbT, slice(None), k), k == 0, k == KD - 1)
                mm.then_inc(q2_ps, 1)

            def scores2(b, g):
                if g == 0:
                    pe.wait_ge(q2_lo, 4 * b + 2)
                    pe.wait_ge(mask_ok, b + 1)
                    pe.wait_ge(k2_ld, 16 * 4 * (b + 1))
                else:
                    pe.wait_ge(sub_ok, 4 * b + g)
                for c in range(2):
                    m = 2 * g + c
                    dst = halves(3 + c)
                    for q in range(QT):
                        pe.matmul(dst[:, q, 0:PAIR], ident_bf[:], mask_bf[:, q].rearrange("p a s -> p (a s)"),
                                  start=(q == 0), stop=False, skip_group_check=True)
                    for q in range(QT):
                        mm = product(dst[:, q, :], both(q2, slice(None), m, slice(q * P, (q + 1) * P)),
                                     both(k2, slice(None), slice(m * PAIR, m * PAIR + W)), False, q == QT - 1,
                                     skip_group_check=True)
                mm.then_inc(s2_ps, 1)

            def transpose2(b, g):
                pe.wait_ge(nrm_ok, 4 * b + g + 1)
                if g == 0:
                    pe.wait_ge(q2_lo, 4 * b + 4)
                else:
                    pe.wait_ge(c2_lo, 4 * b + g)
                for c in range(2):
                    for p in range(2):
                        for q in range(QT):
                            mm = pe.transpose(bank[0:S2, 5 + c, p * T + q * P:p * T + (q + 1) * P],
                                              sc2[g % 2][:, c * QT + q, p, :], ident[:])
                mm.then_inc(t2_ps, 1)

            def weigh2(b, g):
                pe.wait_ge(p2T_ok, 4 * b + g + 1)
                if g == 0:
                    pe.wait_ge(v2_ld, 16 * (b + 1))
                for c in range(2):
                    for j in range(4):
                        col = (2 * g + c) * P + 32 * j
                        mm = pe.matmul(halves(5)[32 * j:32 * j + 32, c, :], v2[:, col:col + 32],
                                       p2T[:, 2 * c + j // 2, :], start=True, stop=True, skip_group_check=True)
                mm.then_inc(c2_ps, 1)

            def output2(b, g):
                if g == 0:
                    pe.wait_ge(y_ok, b)
                pe.wait_ge(c2_hi, 4 * b + g + 1)
                pe.wait_ge(c2_lo, 4 * b + g + 1)
                for c in range(2):
                    m = 2 * g + c
                    for q in range(QT):
                        mm = product(halves(7)[:, q, :], both(c2, slice(None), c, slice(q * P, (q + 1) * P)),
                                     both(wo2, slice(None), m), m == 0 and q == 0, m == XM - 1,
                                     skip_group_check=True)
                mm.then_inc(o2_ps, 1)

            def hidden(b, g):
                if g == 0:
                    pe.wait_ge(xbT_hi, 2 * b + 2)
                    pe.wait_ge(xbT_lo, 2 * b + 2)
                    pe.wait_ge(c2_lo, 4 * b + 4)
                for c in range(2):
                    m = 2 * g + c
                    for k in range(KD):
                        mm = product(halves(3 + g)[:, c, :], both(wfc, slice(None), k, slice(m * P, (m + 1) * P)),
                                     both(xbT, slice(None), k), k == 0, k == KD - 1)
                mm.then_inc(fc_ps, 1)

            def project_down(b, g):
                pe.wait_ge(hid_lo, 4 * b + g + 1)
                for c in range(2):
                    m = 2 * g + c
                    for q in range(QT):
                        mm = product(halves(7)[:, q, :], both(hid, slice(None), m, slice(q * P, (q + 1) * P)),
                                     both(wpj, slice(None), m), m == 0 and q == 0, m == FM - 1,
                                     skip_group_check=True)
                if g == 3:
                    mm.then_inc(y_ps, 1)

            def first():
                pe.wait_ge(const_ok, 8)
                transpose_a(0)
                pe.wait_ge(w_lo, QKV_W + 1)
                project(0, 0)
                project(0, 1)
                project_v(0)

            def step(a, b, n, m):
                A, B, N, M = (e is not None for e in (a, b, n, m))
                if B:
                    for g in range(3):
                        queries(b, g)
                    scores2(b, 0)
                    queries(b, 3)
                if A and not B:
                    for pr in range(XM):
                        keys(pr)
                if A:
                    scores(a, 0)
                    scores(a, 1)
                if B:
                    scores2(b, 1)
                if A:
                    scores(a, 2)
                if A and not B:
                    values2(0)
                if A:
                    scores(a, 3)
                if B:
                    transpose2(b, 0)
                if A:
                    scores(a, 4)
                    scores(a, 5)
                if A and not B:
                    values2(1)
                if B:
                    weigh2(b, 0)
                    scores2(b, 2)
                if A:
                    for h in range(6, 9):
                        scores(a, h)
                if A and not B:
                    values2(2)
                if B:
                    transpose2(b, 1)
                    output2(b, 0)
                if A:
                    scores(a, 9)
                    scores(a, 10)
                if B:
                    weigh2(b, 1)
                    scores2(b, 3)
                if A:
                    scores(a, 11)
                    scores(a, 12)
                if A and not B:
                    values2(3)
                if B:
                    transpose2(b, 2)
                    output2(b, 1)
                if A:
                    scores(a, 13)
                if B:
                    weigh2(b, 2)
                if A:
                    scores(a, 14)
                if A and not B:
                    for v in range(4, VT):
                        values2(v)
                if A:
                    scores(a, 15)
                if B:
                    transpose2(b, 3)
                if A:
                    transpose_max(a)
                if B:
                    output2(b, 2)
                    weigh2(b, 3)
                if N:
                    transpose_a(n)
                if A and not B:
                    lora_up()
                if B:
                    output2(b, 3)
                if A:
                    for h in range(6):
                        shifted(a, h)
                    if N:
                        pe.wait_ge(xaT_lo, n + 1)
                    weigh(a, 0)
                    shifted(a, 6)
                    shifted(a, 7)
                if B:
                    transpose_b(b, 1)
                if A:
                    for h in range(8, 12):
                        shifted(a, h)
                    weigh(a, 1)
                    if not B:
                        lora_down()
                    shifted(a, 12)
                    shifted(a, 13)
                    shifted(a, 14)
                if B:
                    hidden(b, 0)
                if A:
                    shifted(a, 15)
                    weigh(a, 2)
                    weigh(a, 3)
                if B:
                    hidden(b, 1)
                if A:
                    turn_a(a)
                if N:
                    project(n, 0)
                if A:
                    turn_back_a(a)
                if N:
                    project(n, 1)
                if B:
                    hidden(b, 2)
                    hidden(b, 3)
                if A:
                    output_a(a)
                if N:
                    project_v(n)
                if B:
                    project_down(b, 0)
                    project_down(b, 1)
                if A:
                    if not B:
                        pe.wait_ge(w_lo, PJ_W + 1)
                    transpose_b(a, 0)
                if B:
                    project_down(b, 2)
                    project_down(b, 3)

            elements(first, step)(pe)

        @block.scalar
        def _(act):
            def split_hi(k):
                act.wait_ge(raw_sem[k], raw_count[k])
                if k == WQ_W:
                    act.wait_ge(vx_ps, 2 * VT)
                if k == WO2_W:
                    act.wait_ge(kx_st, 16 * 2 * len(K_GROUPS))
                if k == FC_W:
                    act.wait_ge(wstep, 6)
                if k == PJ_W:
                    act.wait_ge(wstep, 12)
                act.activation(split_to[k][0], raw_of[k], ACT.Copy).then_inc(w_hi, 1)

            def keys(m):
                for half in range(2):
                    n = 2 * m + half
                    act.wait_ge(kx_ps, n + 1)
                    act.activation(k_stage[m // KG][0][:, m % KG, half * HS:(half + 1) * HS], bank[:, 3 + n % 4, 0:HS],
                                   ACT.Copy).then_inc(kx_hi, 1)

            def values2(t):
                rows = min(P, NS - t * P)
                if t == 1:
                    act.wait_ge(rot_lo, 2)
                if t >= VR:
                    act.wait_ge(vx_st[t % VR], 16 * (t // VR))
                for half in range(2):
                    n = 2 * t + half
                    act.wait_ge(vx_ps, n + 1)
                    act.activation(v_stage[t % VR][0:rows, half * 512:(half + 1) * 512], bank[0:rows, 3 + n % 4, :],
                                   ACT.Copy).then_inc(vx_ok, 1)

            def copy(dst, src, done):
                act.activation(dst, src, ACT.Copy).then_inc(done, 1)

            def xaT_part(a):
                act.wait_ge(xaT_ps, a + 1)
                act.wait_ge(v_ps, a)
                copy(xaT[0][:].rearrange("p k t -> p (k t)"), bank[:, 2, :], xaT_hi)

            def values(a):
                act.wait_ge(v_ps, a + 1)
                act.wait_ge(pv_ps, 4 * a)
                copy(v_aug[:, :, :, 0:DH], halves(2).rearrange("p q (h d) -> p q h d", h=H), v_ok)

            def rotated(a, w):
                act.wait_ge(rot_ok, 2 * a + w + 1)
                copy(rot_s[0][:, w], rot[:, w], rot_hi)

            def maxima(a):
                act.wait_ge(mT_ps, a + 1)
                act.wait_ge(shift_ld, 32 * a)
                copy(mnegT[:], bank[0:32, 0, 0:T], mT_ok)

            def exponentials(a, n):
                act.wait_ge(st_ps, H * a + n + 1)
                if n < 8:
                    if n == 0:
                        act.wait_ge(pv_ps, 4 * a)
                        act.wait_ge(rot_ok, 2 * a + 2)
                        if isinstance(a, int) and a == 0:
                            for r in range(2, VR):
                                act.wait_ge(vx_st[r], V_STORES[r])
                else:
                    act.wait_ge(pv_ps, 4 * a + n // 4 - 1)
                act.activation(probs[:, n % 8, :], bank[:, shifted_bank(a, n)[1], P:4 * P], ACT.Exp, scale=SCALE).then_inc(p_ok, 1)

            def unnormalised(a, c):
                act.wait_ge(pv_ps, 4 * a + 2 * c + 2)
                if c == 0:
                    act.wait_ge(rot_lo, 2 * a + 2)
                    if isinstance(a, int) and a == 0:
                        act.wait_ge(vx_st[1], V_STORES[1])
                copy(unnorm[:, 2 * c:2 * c + 2], halves(2), u_ok)

            def attention_hi(a):
                act.wait_ge(atT_ps, a + 1)
                copy(attn_s[0].rearrange("p k t -> p (k t)"), bank[:, 0, :], att_hi)

            def xbT_part(b, n):
                act.wait_ge(xbT_ps, 2 * b + n + 1)
                act.wait_ge(fc_ps if n == 0 else q2_ps, 4 * b + 4 * n)
                copy(xbT[0][:].rearrange("p k t -> p (k t)"), bank[:, 7 * n, :], xbT_hi)

            def queries(b, g):
                act.wait_ge(q2_ps, 4 * b + g + 1)
                if g == 0:
                    act.wait_ge(y_ps, b)
                copy(q2[0][:, 2 * g:2 * g + 2], halves(3 + g), q2_hi)

            def exponentials2(b, g):
                act.wait_ge(sub_ok, 4 * b + g + 1)
                act.activation(sc2[g % 2], sc2[g % 2], ACT.Exp, scale=XSCALE).then_inc(e2_ok, 1)

            def probabilities2(b, g):
                act.wait_ge(t2_ps, 4 * b + g + 1)
                if g == 0:
                    act.wait_ge(hid_lo, 4 * b)
                else:
                    act.wait_ge(c2_ps, 4 * b + g)
                copy(p2T.rearrange("p (c a) t -> p c (a t)", c=2), bank[0:S2, 5:7, :], p2T_ok)

            def context_hi(b, g):
                act.wait_ge(c2_ps, 4 * b + g + 1)
                act.wait_ge(o2_ps, 4 * b + g)
                copy(c2[0][:], halves(5), c2_hi)

            def hidden(b, g):
                act.wait_ge(fc_ps, 4 * b + g + 1)
                if g == 0:
                    act.wait_ge(c2_ps, 4 * b + 4)
                    act.wait_ge(s2_ps, 4 * b + 4)
                if g >= 2:
                    act.wait_ge(hid_lo, 4 * b + g - 1)
                for c in range(2):
                    m = 2 * g + c
                    last = act.activation(gl[:, g % 2, c, :], halves(3 + g)[:, c, :], ACT.Gelu,
                                          bias=bfc_t[:, m:m + 1])
                last.then_inc(gl_ok, 1)
                act.wait_ge(gl_ok, 4 * b + g + 1)
                copy(hid[0][:, 2 * g:2 * g + 2], gl[:, g % 2], hid_hi)

            def first():
                xaT_part(0)
                split_hi(QKV_W)
                split_hi(WK_W)
                split_hi(CTX_W)
                rotated(0, 0)
                rotated(0, 1)
                values(0)
                act.wait_ge(const_ld, 16 * 4)

            def step(a, b, n, m):
                A, B, N, M = (e is not None for e in (a, b, n, m))
                if B:
                    for g in range(3):
                        queries(b, g)
                    exponentials2(b, 0)
                    queries(b, 3)
                    exponentials2(b, 1)
                    probabilities2(b, 0)
                    context_hi(b, 0)
                    exponentials2(b, 2)
                    probabilities2(b, 1)
                    context_hi(b, 1)
                    probabilities2(b, 2)
                    exponentials2(b, 3)
                    context_hi(b, 2)
                if A and not B:
                    for pr in range(XM // 2):
                        keys(pr)
                    split_hi(WV_W)
                    split_hi(WO_W)
                    for pr in range(XM // 2, XM):
                        keys(pr)
                    for t in range(VT):
                        values2(t)
                if B:
                    probabilities2(b, 3)
                if A:
                    maxima(a)
                if B:
                    context_hi(b, 3)
                if N:
                    xaT_part(n)
                if A and not B:
                    split_hi(WO2_W)
                if A:
                    for h in range(4):
                        exponentials(a, h)
                if A and not B:
                    split_hi(FC_W)
                if A:
                    for h in range(4, 8):
                        exponentials(a, h)
                if A and not B:
                    split_hi(WQ_W)
                if B:
                    xbT_part(b, 1)
                if A:
                    for h in range(8, 12):
                        exponentials(a, h)
                    unnormalised(a, 0)
                    for h in range(12, 16):
                        exponentials(a, h)
                    unnormalised(a, 1)
                if A and not B:
                    split_hi(PJ_W)
                if B:
                    hidden(b, 0)
                if A:
                    attention_hi(a)
                if N:
                    rotated(n, 0)
                if B:
                    hidden(b, 1)
                if N:
                    rotated(n, 1)
                if B:
                    hidden(b, 2)
                    hidden(b, 3)
                if N:
                    values(n)
                if A:
                    xbT_part(a, 0)

            elements(first, step)(act)

        @block.vector
        def _(dve):
            def split_lo(k):
                dve.wait_ge(w_hi, k + 1)
                dve.tensor_tensor(split_to[k][1], raw_of[k], split_to[k][0].bitcast(F32),
                                  ALU.subtract).then_inc(w_lo, 1)

            def largest(n, k):
                dve.wait_ge(raw_sem[k], raw_count[k])
                dve.tensor_reduce(wmax[:, 0:1], raw_of[k], AX_X, ALU.max,
                                  apply_absolute_value=True).then_inc(wmax_ok, 1)

            def scale(n, k):
                dve.wait_ge(wmax_all, n + 1)
                dve.tensor_scalar(wscale[:, n:n + 1], wmax[:, 1:2], 1.0 / QMAX, None, ALU.mult).then_inc(wstep, 1)
                dve.wait_ge(wstep, 6 * n + 1)
                dve.reciprocal(winv[:, n:n + 1], wscale[:, n:n + 1]).then_inc(wstep, 1)

            def quantise(n, k, part):
                w = raw_of[k]
                dve.wait_ge(wstep, 6 * n + 2 + part)
                if part == 0:
                    dve.tensor_scalar(w, w, winv[:, n:n + 1], ROUND, ALU.mult, ALU.add).then_inc(wstep, 1)
                elif part == 1:
                    dve.tensor_scalar(w, w, ROUND, QMAX, ALU.subtract, ALU.min).then_inc(wstep, 1)
                else:
                    dve.tensor_scalar(w, w, -QMAX - 1.0, wscale[:, n:n + 1], ALU.max, ALU.mult).then_inc(wstep, 1)

            def add_lora(n, k):
                w = raw_of[k]
                dve.wait_ge(wstep, 6 * n + 5)
                dve.wait_ge(lora_ps, n + 1)
                dve.scalar_tensor_tensor(out=w, in0=bank[:, 3:7, :].rearrange("p b n -> p (b n)"), scalar=LORA_SCALE,
                                         in1=w, op0=ALU.mult, op1=ALU.add).then_inc(wstep, 1)

            def keys(m):
                for half in range(2):
                    n = 2 * m + half
                    hi, lo = (v[:, m % KG, half * HS:(half + 1) * HS] for v in k_stage[m // KG])
                    dve.wait_ge(kx_hi, n + 1)
                    dve.tensor_tensor(lo, bank[:, 3 + n % 4, 0:HS], hi.bitcast(F32), ALU.subtract).then_inc(kx_lo, 1)

            def statistics(src, st, mv, rs, sems, ve_ok, n):
                st_ok, mv_ok, rs_ok, xn_ok = sems
                for q in range(QT):
                    last = dve.bn_stats(st[:, q, :], src[:, q, :])
                last.then_inc(st_ok, 1)
                dve.wait_ge(st_ok, n + 1)
                dve.sem_inc(waited_dve, 1)
                for q in range(QT):
                    last = dve.bn_aggr(mv[:, q, :], st[:, q, :])
                last.then_inc(mv_ok, 1)
                dve.wait_ge(mv_ok, n + 1)
                dve.tensor_scalar(rs[:], mv[:, :, 1:2], EPS, None, ALU.add).then_inc(ve_ok, 1)

            def norm(src, xn, mv, rs, sems, n):
                st_ok, mv_ok, rs_ok, xn_ok = sems
                dve.wait_ge(rs_ok, n + 1)
                for q in range(QT):
                    last = dve.tensor_scalar(xn[:, q, :], src[:, q, :], mv[:, q, 0:1], rs[:, q, :],
                                             ALU.subtract, ALU.mult)
                last.then_inc(xn_ok, 1)

            def low(dst, src, hi, done):
                dve.tensor_tensor(dst, src, hi.bitcast(F32), ALU.subtract).then_inc(done, 1)

            sems_a = (lna_st, lna_mv, lna_rs, xn_a_ok)
            sems_b = (lnb_st, lnb_mv, lnb_rs, xn_b_ok)

            def statistics_a(a):
                dve.wait_ge(x_ld, 16 * (a + 1))
                statistics(x_in, st_a, mv_a, rs_a, sems_a, lna_ve, a)

            def norm_a(a):
                dve.wait_ge(xaT_ps, a)
                norm(x_in, xn_a, mv_a, rs_a, sems_a, a)

            def xaT_part(a):
                dve.wait_ge(xaT_hi, a + 1)
                low(xaT[1][:].rearrange("p k t -> p (k t)"), bank[:, 2, :],
                    xaT[0][:].rearrange("p k t -> p (k t)"), xaT_lo)

            def rotary(a, w):
                dve.wait_ge(qk_ps, 2 * a + w + 1)
                if w == 0:
                    dve.wait_ge(pv_ps, 4 * a)
                    dve.wait_ge(const_ld, 16 * 4)
                else:
                    dve.wait_ge(rot_ok, 2 * a + w)
                for dst, table in ((tcos, cos_t), (tsin, sin_t)):
                    last = dve.tensor_tensor(dst, halves(2 - w),
                                             table[:].rearrange("p t -> p () t").broadcast_to([P, 2, T]), ALU.mult)
                last.then_inc(trig, 1)

            def maxima(a, h):
                dve.wait_ge(s_ps, H * a + h + 1)
                if h == 0:
                    dve.wait_ge(m_split, 2 * a)
                for q in range(QT):
                    off = (1 - q) * W
                    last = dve.tensor_reduce(mneg[:, q, h % 2, h // 2:h // 2 + 1], bank[:, h % 3, off:off + (q + 1) * P],
                                             AX_X, ALU.max, negate=True)
                last.then_inc(s_max, 1)

            def split_max(a):
                dve.wait_ge(s_max, H * a + H)
                dve.wait_ge(mT_ps, a)
                dve.tensor_copy(mneg_s[:, :, :, 0, :], mneg[:]).then_inc(m_split, 1)
                dve.wait_ge(m_split, 2 * a + 1)
                low(mneg_s[:, :, :, 1, :], mneg[:], mneg_s[:, :, :, 0, :], m_split)

            def attention(a):
                dve.wait_ge(ut_ps, a + 1)
                u = bank[:, 0:QT, :].rearrange("p q (h e) -> p q h e", h=H)
                dve.reciprocal(rc_a[:], u[:, :, :, DH]).then_inc(rca_ok, 1)
                dve.wait_ge(rca_ok, a + 1)
                for q in range(QT):
                    last = dve.tensor_tensor(attn[:, q, :].rearrange("p (h d) -> p h d", h=H), u[:, q, :, 0:DH],
                                             rc_a[:, q].rearrange("p h -> p h ()").broadcast_to([P, H, DH]), ALU.mult)
                last.then_inc(att_ok, 1)

            def attention_lo(a):
                dve.wait_ge(att_hi, a + 1)
                low(attn_s[1].rearrange("p k t -> p (k t)"), bank[:, 0, :],
                    attn_s[0].rearrange("p k t -> p (k t)"), att_lo)

            def residual_a(a):
                dve.wait_ge(o_ps, a + 1)
                dve.wait_ge(xres_ld, 16 * (a + 1))
                dve.wait_ge(x2_ok, a)
                dve.tensor_tensor(x1[:], halves(0), x_res[:], ALU.add).then_inc(x1_ok, 1)

            def mask_bias(b):
                dve.wait_ge(mask_ld, 16 * (b + 1))
                dve.wait_ge(s2_ps, 4 * b)
                for q in range(QT):
                    last = dve.tensor_scalar(mask_bf[:, q], mask_u8[:, q:q + 1, :].broadcast_to([P, 2, S2]),
                                             NEG, None, ALU.mult)
                last.then_inc(mask_ok, 1)

            def statistics_b(b, n):
                dve.wait_ge(x1_ok if n == 0 else x2_ok, b + 1)
                statistics(x1 if n == 0 else x2, st_b, mv_b, rs_b, sems_b, lnb_ve, 2 * b + n)

            def norm_b(b, n):
                dve.wait_ge(xbT_ps, 2 * b + n)
                norm(x1 if n == 0 else x2, xn_b, mv_b, rs_b, sems_b, 2 * b + n)

            def xbT_part(b, n):
                dve.wait_ge(xbT_hi, 2 * b + n + 1)
                low(xbT[1][:].rearrange("p k t -> p (k t)"), bank[:, 7 * n, :],
                    xbT[0][:].rearrange("p k t -> p (k t)"), xbT_lo)

            def queries(b, g):
                dve.wait_ge(q2_hi, 4 * b + g + 1)
                low(q2[1][:, 2 * g:2 * g + 2], halves(3 + g), q2[0][:, 2 * g:2 * g + 2], q2_lo)

            def softmax2(b, g):
                r = g % 2
                dve.wait_ge(s2_ps, 4 * b + g + 1)
                ps = bank[:, 3:5, :].rearrange("p c (q n) -> p (c q) n", q=2)[:, :, 0:PAIR] \
                    .rearrange("p g (a s) -> p g a s", a=2)
                dve.tensor_reduce(mx2[:, r], ps, AX_X, ALU.max).then_inc(mx2_ok, 1)
                dve.wait_ge(mx2_ok, 4 * b + g + 1)
                if g < 2:
                    dve.wait_ge(t2_ps, 4 * b)
                else:
                    dve.wait_ge(t2_ps, 4 * b + g - 1)
                dve.tensor_tensor(sc2[r], ps, mx2[:, r].rearrange("p g a -> p g a ()").broadcast_to([P, 4, 2, S2]),
                                  ALU.subtract).then_inc(sub_ok, 1)

            def sums2(b, g):
                r = g % 2
                dve.wait_ge(e2_ok, 4 * b + g + 1)
                dve.tensor_reduce(sm2[:, r], sc2[r], AX_X, ALU.add).then_inc(sm2_ok, 1)
                dve.wait_ge(sm2_ok, 4 * b + g + 1)
                dve.reciprocal(rc2[:, r], sm2[:, r]).then_inc(rc2_ok, 1)

            def context_lo(b, g):
                dve.wait_ge(c2_hi, 4 * b + g + 1)
                low(c2[1][:], halves(5), c2[0][:], c2_lo)

            def residual_b(b):
                dve.wait_ge(o2_ps, 4 * b + 4)
                dve.wait_ge(x2b_ok, b)
                dve.tensor_tensor(x2[:], halves(7), x1[:], ALU.add).then_inc(x2_ok, 1)

            def hidden_lo(b, g):
                dve.wait_ge(hid_hi, 4 * b + g + 1)
                low(hid[1][:, 2 * g:2 * g + 2], gl[:, g % 2], hid[0][:, 2 * g:2 * g + 2], hid_lo)

            def result(b):
                dve.wait_ge(y_ps, b + 1)
                dve.wait_ge(x2b_ok, b + 1)
                dve.wait_ge(y_st, 16 * b)
                dve.tensor_tensor(y, halves(7), x2b, ALU.add).then_inc(y_ok, 1)

            def first():
                statistics_a(0)
                norm_a(0)
                xaT_part(0)
                split_lo(QKV_W)
                split_lo(WK_W)
                rotary(0, 0)
                rotary(0, 1)
                split_lo(CTX_W)
                statistics_a(1)
                norm_a(1)

            def step(a, b, n, m):
                A, B, N, M = (e is not None for e in (a, b, n, m))
                if B:
                    mask_bias(b)
                    for g in range(3):
                        queries(b, g)
                    softmax2(b, 0)
                if A and not B:
                    for pr in range(XM // 2):
                        keys(pr)
                    split_lo(WV_W)
                    split_lo(WO_W)
                    for pr in range(XM // 2, XM):
                        keys(pr)
                if A:
                    maxima(a, 0)
                if A and not B:
                    largest(0, FC_W)
                if B:
                    sums2(b, 0)
                    queries(b, 3)
                    softmax2(b, 1)
                if A:
                    for h in range(1, 4):
                        maxima(a, h)
                if B:
                    sums2(b, 1)
                if A:
                    maxima(a, 4)
                    maxima(a, 5)
                if A and not B:
                    scale(0, FC_W)
                if B:
                    context_lo(b, 0)
                    softmax2(b, 2)
                if A:
                    for h in range(6, 9):
                        maxima(a, h)
                if A and not B:
                    quantise(0, FC_W, 0)
                if B:
                    sums2(b, 2)
                if A:
                    maxima(a, 9)
                    maxima(a, 10)
                if A and not B:
                    quantise(0, FC_W, 1)
                if B:
                    context_lo(b, 1)
                    softmax2(b, 3)
                if A:
                    maxima(a, 11)
                    maxima(a, 12)
                if B:
                    sums2(b, 3)
                if A:
                    maxima(a, 13)
                if A and not B:
                    quantise(0, FC_W, 2)
                if A:
                    maxima(a, 14)
                if B:
                    context_lo(b, 2)
                if A:
                    maxima(a, 15)
                    split_max(a)
                if B:
                    context_lo(b, 3)
                if N:
                    xaT_part(n)
                if B:
                    residual_b(b)
                    statistics_b(b, 1)
                    norm_b(b, 1)
                    xbT_part(b, 1)
                if A and not B:
                    add_lora(0, FC_W)
                    split_lo(WO2_W)
                    split_lo(FC_W)
                if M:
                    statistics_a(m)
                    norm_a(m)
                if A and not B:
                    split_lo(WQ_W)
                    largest(1, PJ_W)
                    scale(1, PJ_W)
                    for part in range(3):
                        quantise(1, PJ_W, part)
                    add_lora(1, PJ_W)
                if A:
                    attention(a)
                if N:
                    rotary(n, 0)
                if A:
                    attention_lo(a)
                if A and not B:
                    split_lo(PJ_W)
                if N:
                    rotary(n, 1)
                if B:
                    hidden_lo(b, 0)
                    hidden_lo(b, 1)
                if A:
                    residual_a(a)
                    statistics_b(a, 0)
                    norm_b(a, 0)
                if B:
                    hidden_lo(b, 2)
                    hidden_lo(b, 3)
                if A:
                    xbT_part(a, 0)
                if B:
                    result(b)

            elements(first, step)(dve)


IN_ORDER = ["x", "ctxT", "mask", "wqT", "wkT", "wvT", "woT", "wQ", "wK", "wV", "wO", "wfcT", "bfc", "Afc", "BfcT",
            "wpjT", "bpj", "Apj", "BpjT", "cos", "sin"]


def rotary_tables(tokens, head_width, repeat):
    half = head_width // 2
    theta = np.float32(10000.0) ** (np.float32(-2.0) * np.arange(half, dtype=np.float32) / np.float32(head_width))
    angles = np.arange(tokens, dtype=np.float32)[None, :] * theta.astype(np.float32)[:, None]
    rows = [np.tile(np.repeat(f(angles).astype(np.float32), repeat, axis=0), (2, 1)) for f in (np.cos, np.sin)]
    return rows


def kernel(x, ctx_1024, mask_BxSxS2_bk1, L0_attn_W_q, L0_attn_W_k, L0_attn_W_v, L0_attn_W_o, L0_xattn_W_Q,
           L0_xattn_W_K, L0_xattn_W_V, L0_xattn_W_O, L0_ffn_W_fc, L0_ffn_b_fc, L0_ffn_A_fc, L0_ffn_B_fc,
           L0_ffn_W_proj, L0_ffn_b_proj, L0_ffn_A_proj, L0_ffn_B_proj):
    import concourse.bacc as bacc
    from concourse.bass_utils import run_bass_kernel_spmd

    H = 16
    nb, tokens, d = x.shape
    hw = d // H

    def rotary_order(w):
        w = np.asarray(w).reshape(H // 2, 2, hw // 2, 2, d)
        return w.transpose(4, 3, 1, 2, 0).reshape(d, d)

    cos, sin = rotary_tables(tokens, hw, H // 2)
    f = L0_ffn_W_fc.shape[0]
    laid = {
        "x": x, "ctxT": np.asarray(ctx_1024).transpose(2, 0, 1).reshape(d, -1),
        "mask": np.asarray(mask_BxSxS2_bk1),
        "wqT": rotary_order(L0_attn_W_q), "wkT": rotary_order(L0_attn_W_k),
        "wvT": np.asarray(L0_attn_W_v).T, "woT": np.asarray(L0_attn_W_o).T,
        "wQ": L0_xattn_W_Q, "wK": L0_xattn_W_K, "wV": L0_xattn_W_V, "wO": L0_xattn_W_O,
        "wfcT": np.asarray(L0_ffn_W_fc).T, "bfc": np.asarray(L0_ffn_b_fc).reshape(f // P, P).T,
        "Afc": L0_ffn_A_fc, "BfcT": np.asarray(L0_ffn_B_fc).T,
        "wpjT": np.asarray(L0_ffn_W_proj).T, "bpj": np.asarray(L0_ffn_b_proj).reshape(1, d),
        "Apj": L0_ffn_A_proj, "BpjT": np.asarray(L0_ffn_B_proj).T, "cos": cos, "sin": sin,
    }
    nc = bacc.Bacc("TRN2", target_bir_lowering=False, num_devices=1)
    arrays, args = {}, []
    for name in IN_ORDER:
        a = np.ascontiguousarray(laid[name])
        arrays[f"in_{name}"] = a
        args.append(nc.dram_tensor(f"in_{name}", a.shape, mybir.dt.from_np(a.dtype), kind="ExternalInput").ap())
    out = nc.dram_tensor("out_y", x.shape, F32, kind="ExternalOutput").ap()
    decoder_layer(nc, *args, out)
    r = run_bass_kernel_spmd(nc, [arrays], core_ids=[0])
    return r.results[0]["out_y"]
```
